# Optimizing a Trainium2 kernel written in Bass

```python
import numpy as np
import jax
import jax.numpy as jnp

def _softmax(x, axis=-1):
    return jax.nn.softmax(x, axis=axis)

def _gelu(x):
    return jax.nn.gelu(x, approximate=True)

def _silu(x):
    return jax.nn.silu(x)

def _sigmoid(x):
    return jax.nn.sigmoid(x)

def _layernorm(x, axis=-1, eps=1e-05):
    m = jnp.mean(x, axis=axis, keepdims=True)
    v = jnp.var(x, axis=axis, keepdims=True)
    return (x - m) / jnp.sqrt(v + eps)

def _scatter_add(tgt, idx, src, axis=0):
    return tgt.at[idx].add(src)

def _segment_sum(src, seg, n):
    return jax.ops.segment_sum(src, seg, n)
kernel_name = 'mk_gnn_preln_d4_gnn_r8_c975e9'

def setup_inputs(seed: int=0):
    np.random.seed(seed)
    _w = jnp.asarray

    def _rec_inputs():
        import jax
        import jax.numpy as jnp
        _gk = jax.random.key(seed)
        x = -0.000202 + 1 * jax.random.normal(jax.random.fold_in(_gk, 1), (12500, 64), jnp.float32)
        src = jax.random.randint(jax.random.fold_in(_gk, 2), (200000,), 0, 12500, jnp.int32)
        dst = jnp.minimum((12500 * jax.random.uniform(jax.random.fold_in(_gk, 3), (200000,)) ** 2.0).astype(jnp.int32), 99999)
        _o = jnp.argsort(dst, stable=True)
        src = src[_o]
        dst = dst[_o]
        edge_attr_32 = -9.77346e-05 + 0.999888 * jax.random.normal(jax.random.fold_in(_gk, 12), (200000, 32), jnp.float32)
        edge_attr_64 = -8.16379e-05 + 0.999858 * jax.random.normal(jax.random.fold_in(_gk, 13), (200000, 64), jnp.float32)
        return (x, src, dst, edge_attr_32, edge_attr_64)
    x, src, dst, edge_attr_32, edge_attr_64 = _rec_inputs()

    def _L0_gnn_setup():
        import jax, jax.numpy as jnp
        import numpy as np
        N_NODES = 12500
        N_EDGES = 200000
        D_IN = 64
        D_HID = 64
        D_OUT = 64

        def _gcn_norm(edge_index, num_nodes, dtype):
            loop = jnp.arange(num_nodes, dtype=edge_index.dtype)
            src = jnp.concatenate([edge_index[0], loop])
            dst = jnp.concatenate([edge_index[1], loop])
            deg = jax.ops.segment_sum(jnp.ones(src.shape[0], dtype=dtype), dst, num_segments=num_nodes)
            dis = jax.lax.rsqrt(jnp.maximum(deg, 1.0))
            norm = dis[src] * dis[dst]
            return (src, dst, norm)

        def _gcn_layer(x, src, dst, norm, W, b, num_nodes):
            h = x @ W
            msg = h[src] * norm[:, None]
            agg = jax.ops.segment_sum(msg, dst, num_segments=num_nodes)
            return agg + b
        key = jax.random.key(seed)
        ks = jax.random.split(key, 12)
        x = jax.random.normal(ks[0], (N_NODES, D_IN), dtype=jnp.float32)
        edge_index = jax.random.randint(ks[1], (2, N_EDGES), 0, N_NODES, dtype=jnp.int64)

        def glorot(k, fan_in, fan_out):
            s = jnp.sqrt(6.0 / (fan_in + fan_out))
            return jax.random.uniform(k, (fan_in, fan_out), jnp.float32, -s, s)
        return {'x': x, 'edge_index': edge_index, 'W1': glorot(ks[2], D_IN, D_HID), 'b1': jnp.zeros((D_HID,), jnp.float32), 'W2': glorot(ks[3], D_HID, D_HID), 'b2': jnp.zeros((D_HID,), jnp.float32), 'W3': glorot(ks[4], D_HID, D_HID), 'b3': jnp.zeros((D_HID,), jnp.float32), 'W4': glorot(ks[5], D_HID, D_OUT), 'b4': jnp.zeros((D_OUT,), jnp.float32)}
    _L0_gnn_all = _L0_gnn_setup()
    _L0_gnn_in = {k: v for k, v in _L0_gnn_all.items() if k in ('W1', 'b1', 'W2', 'b2', 'W3', 'b3', 'W4', 'b4')}
    del _L0_gnn_all

    def _L1_gnn_setup():
        import jax, jax.numpy as jnp
        import numpy as np
        N_NODES = 6250
        N_EDGES = 200000
        NODE_DIM = 64
        EDGE_DIM = 32
        UNITS = 64

        def _glorot(key, shape):
            fan_in, fan_out = (shape[0], shape[1])
            lim = jnp.sqrt(6.0 / (fan_in + fan_out))
            return jax.random.uniform(key, shape, jnp.float32, -lim, lim)
        key = jax.random.key(seed)
        ks = jax.random.split(key, 16)
        msg_in = 2 * NODE_DIM + EDGE_DIM
        upd_in = NODE_DIM + UNITS
        return {'node_features': jax.random.normal(ks[0], (N_NODES, NODE_DIM), jnp.float32), 'edge_features': jax.random.normal(ks[1], (N_EDGES, EDGE_DIM), jnp.float32), 'senders': jax.random.randint(ks[2], (N_EDGES,), 0, N_NODES, jnp.int32), 'receivers': jnp.sort(jax.random.randint(ks[3], (N_EDGES,), 0, N_NODES, jnp.int32)), 'W1': _glorot(ks[4], (msg_in, UNITS)), 'b1': jnp.zeros((UNITS,), jnp.float32), 'W2': _glorot(ks[5], (UNITS, UNITS)), 'b2': jnp.zeros((UNITS,), jnp.float32), 'Wa1': _glorot(ks[6], (msg_in, UNITS)), 'ba1': jnp.zeros((UNITS,), jnp.float32), 'Wa2': _glorot(ks[7], (UNITS, 1)), 'ba2': jnp.zeros((1,), jnp.float32), 'Wu1': _glorot(ks[8], (upd_in, UNITS)), 'bu1': jnp.zeros((UNITS,), jnp.float32), 'Wu2': _glorot(ks[9], (UNITS, UNITS)), 'bu2': jnp.zeros((UNITS,), jnp.float32)}
    _L1_gnn_all = _L1_gnn_setup()
    _L1_gnn_in = {k: v for k, v in _L1_gnn_all.items() if k in ('W1', 'b1', 'W2', 'b2', 'Wa1', 'ba1', 'Wa2', 'ba2', 'Wu1', 'bu1', 'Wu2', 'bu2')}
    del _L1_gnn_all

    def _L2_gnn_setup():
        import jax, jax.numpy as jnp
        import numpy as np
        N_NODES = 12500
        N_EDGES = 200000
        INPUT_DIM = 64
        H_DIM = 1
        key = jax.random.key(seed)
        k_h, k_src, k_dst, k_w, k_b = jax.random.split(key, 5)
        h = jax.random.normal(k_h, (N_NODES, INPUT_DIM), dtype=jnp.float32)
        src = jax.random.randint(k_src, (N_EDGES,), 0, N_NODES, dtype=jnp.int32)
        dst = jax.random.randint(k_dst, (N_EDGES,), 0, N_NODES, dtype=jnp.int32)
        W = jax.random.normal(k_w, (H_DIM, 2 * INPUT_DIM), dtype=jnp.float32) * 0.1
        b = jax.random.normal(k_b, (H_DIM,), dtype=jnp.float32) * 0.1
        return {'h': h, 'src': src, 'dst': dst, 'W': W, 'b': b}
    _L2_gnn_all = _L2_gnn_setup()
    _L2_gnn_in = {k: v for k, v in _L2_gnn_all.items() if k in ('W', 'b')}
    del _L2_gnn_all

    def _L3_gnn_setup():
        import jax, jax.numpy as jnp
        import numpy as np
        N = 12500
        NE = 200000
        IN_DIM = 64
        OUT_DIM = 64
        H = 8
        D = OUT_DIM // H
        key = jax.random.key(seed)
        ks = jax.random.split(key, 12)
        s = 1.0 / np.sqrt(IN_DIM)
        x = jax.random.normal(ks[0], (N, IN_DIM), jnp.float32)
        edge_attr = jax.random.normal(ks[1], (NE, IN_DIM), jnp.float32)
        edge_index = jax.random.randint(ks[2], (2, NE), 0, N, dtype=jnp.int32)
        WQ = jax.random.normal(ks[3], (IN_DIM, OUT_DIM), jnp.float32) * s
        WK = jax.random.normal(ks[4], (IN_DIM, OUT_DIM), jnp.float32) * s
        WE = jax.random.normal(ks[5], (IN_DIM, OUT_DIM), jnp.float32) * s
        WV = jax.random.normal(ks[6], (IN_DIM, OUT_DIM), jnp.float32) * s
        bQ = jax.random.normal(ks[7], (OUT_DIM,), jnp.float32) * 0.01
        bK = jax.random.normal(ks[8], (OUT_DIM,), jnp.float32) * 0.01
        bE = jax.random.normal(ks[9], (OUT_DIM,), jnp.float32) * 0.01
        bV = jax.random.normal(ks[10], (OUT_DIM,), jnp.float32) * 0.01
        return {'x': x, 'edge_attr': edge_attr, 'edge_index': edge_index, 'WQ': WQ, 'bQ': bQ, 'WK': WK, 'bK': bK, 'WE': WE, 'bE': bE, 'WV': WV, 'bV': bV}
    _L3_gnn_all = _L3_gnn_setup()
    _L3_gnn_in = {k: v for k, v in _L3_gnn_all.items() if k in ('WQ', 'bQ', 'WK', 'bK', 'WE', 'bE', 'WV', 'bV')}
    del _L3_gnn_all
    return {'x': x, 'src': src, 'dst': dst, 'edge_attr_32': edge_attr_32, 'edge_attr_64': edge_attr_64, 'L0_gnn_W1': _L0_gnn_in['W1'], 'L0_gnn_b1': _L0_gnn_in['b1'], 'L0_gnn_W2': _L0_gnn_in['W2'], 'L0_gnn_b2': _L0_gnn_in['b2'], 'L0_gnn_W3': _L0_gnn_in['W3'], 'L0_gnn_b3': _L0_gnn_in['b3'], 'L0_gnn_W4': _L0_gnn_in['W4'], 'L0_gnn_b4': _L0_gnn_in['b4'], 'L1_gnn_W1': _L1_gnn_in['W1'], 'L1_gnn_b1': _L1_gnn_in['b1'], 'L1_gnn_W2': _L1_gnn_in['W2'], 'L1_gnn_b2': _L1_gnn_in['b2'], 'L1_gnn_Wa1': _L1_gnn_in['Wa1'], 'L1_gnn_ba1': _L1_gnn_in['ba1'], 'L1_gnn_Wa2': _L1_gnn_in['Wa2'], 'L1_gnn_ba2': _L1_gnn_in['ba2'], 'L1_gnn_Wu1': _L1_gnn_in['Wu1'], 'L1_gnn_bu1': _L1_gnn_in['bu1'], 'L1_gnn_Wu2': _L1_gnn_in['Wu2'], 'L1_gnn_bu2': _L1_gnn_in['bu2'], 'L2_gnn_W': _L2_gnn_in['W'], 'L2_gnn_b': _L2_gnn_in['b'], 'L3_gnn_WQ': _L3_gnn_in['WQ'], 'L3_gnn_bQ': _L3_gnn_in['bQ'], 'L3_gnn_WK': _L3_gnn_in['WK'], 'L3_gnn_bK': _L3_gnn_in['bK'], 'L3_gnn_WE': _L3_gnn_in['WE'], 'L3_gnn_bE': _L3_gnn_in['bE'], 'L3_gnn_WV': _L3_gnn_in['WV'], 'L3_gnn_bV': _L3_gnn_in['bV']}

def reference(x, src, dst, edge_attr_32, edge_attr_64, L0_gnn_W1, L0_gnn_b1, L0_gnn_W2, L0_gnn_b2, L0_gnn_W3, L0_gnn_b3, L0_gnn_W4, L0_gnn_b4, L1_gnn_W1, L1_gnn_b1, L1_gnn_W2, L1_gnn_b2, L1_gnn_Wa1, L1_gnn_ba1, L1_gnn_Wa2, L1_gnn_ba2, L1_gnn_Wu1, L1_gnn_bu1, L1_gnn_Wu2, L1_gnn_bu2, L2_gnn_W, L2_gnn_b, L3_gnn_WQ, L3_gnn_bQ, L3_gnn_WK, L3_gnn_bK, L3_gnn_WE, L3_gnn_bE, L3_gnn_WV, L3_gnn_bV):
    import jax
    import jax.numpy as jnp

    def _L0_gnn_ref(x, edge_index, W1, b1, W2, b2, W3, b3, W4, b4):
        import jax, jax.numpy as jnp
        import numpy as np
        N_NODES = 12500
        N_EDGES = 200000
        D_IN = 64
        D_HID = 64
        D_OUT = 64

        def _gcn_norm(edge_index, num_nodes, dtype):
            loop = jnp.arange(num_nodes, dtype=edge_index.dtype)
            src = jnp.concatenate([edge_index[0], loop])
            dst = jnp.concatenate([edge_index[1], loop])
            deg = jax.ops.segment_sum(jnp.ones(src.shape[0], dtype=dtype), dst, num_segments=num_nodes)
            dis = jax.lax.rsqrt(jnp.maximum(deg, 1.0))
            norm = dis[src] * dis[dst]
            return (src, dst, norm)

        def _gcn_layer(x, src, dst, norm, W, b, num_nodes):
            h = x @ W
            msg = h[src] * norm[:, None]
            agg = jax.ops.segment_sum(msg, dst, num_segments=num_nodes)
            return agg + b
        N = x.shape[0]
        src, dst, norm = _gcn_norm(edge_index, N, x.dtype)
        x = jax.nn.relu(_gcn_layer(x, src, dst, norm, W1, b1, N))
        x = jax.nn.relu(_gcn_layer(x, src, dst, norm, W2, b2, N))
        x = jax.nn.relu(_gcn_layer(x, src, dst, norm, W3, b3, N))
        x = _gcn_layer(x, src, dst, norm, W4, b4, N)
        return x

    def _L1_gnn_ref(node_features, edge_features, senders, receivers, W1, b1, W2, b2, Wa1, ba1, Wa2, ba2, Wu1, bu1, Wu2, bu2):
        import jax, jax.numpy as jnp
        import numpy as np
        N_NODES = 6250
        N_EDGES = 200000
        NODE_DIM = 64
        EDGE_DIM = 32
        UNITS = 64

        def _glorot(key, shape):
            fan_in, fan_out = (shape[0], shape[1])
            lim = jnp.sqrt(6.0 / (fan_in + fan_out))
            return jax.random.uniform(key, shape, jnp.float32, -lim, lim)
        act = jax.nn.swish
        msg_in = jnp.concatenate([node_features[senders], node_features[receivers], edge_features], axis=-1)
        messages = act(msg_in @ W1 + b1) @ W2 + b2
        att_logits = act(msg_in @ Wa1 + ba1) @ Wa2 + ba2
        att = jax.nn.softmax(att_logits, axis=0)
        messages = messages * att
        aggregated = jax.ops.segment_sum(messages, receivers, num_segments=node_features.shape[0])
        upd_in = jnp.concatenate([node_features, aggregated], axis=-1)
        return act(upd_in @ Wu1 + bu1) @ Wu2 + bu2

    def _L2_gnn_ref(h, src, dst, W, b):
        import jax, jax.numpy as jnp
        import numpy as np
        N_NODES = 12500
        N_EDGES = 200000
        INPUT_DIM = 64
        H_DIM = 1
        n = h.shape[0]
        x = jnp.concatenate([h[src], h[dst]], axis=-1)
        e = jax.nn.leaky_relu(x @ W.T + b)
        e_max = jax.ops.segment_max(e, dst, num_segments=n)
        e_exp = jnp.exp(e - e_max[dst])
        e_sum = jax.ops.segment_sum(e_exp, dst, num_segments=n)
        alpha = e_exp / e_sum[dst]
        out = jax.ops.segment_sum(h[src] * alpha, dst, num_segments=n)
        return out

    def _L3_gnn_ref(x, edge_attr, edge_index, WQ, bQ, WK, bK, WE, bE, WV, bV):
        import jax, jax.numpy as jnp
        import numpy as np
        N = 12500
        NE = 200000
        IN_DIM = 64
        OUT_DIM = 64
        H = 8
        D = OUT_DIM // H
        n = x.shape[0]
        Qh = (x @ WQ + bQ).reshape(n, H, D)
        Kh = (x @ WK + bK).reshape(n, H, D)
        Vh = (x @ WV + bV).reshape(n, H, D)
        Eh = (edge_attr @ WE + bE).reshape(-1, H, D)
        src = edge_index[0]
        dst = edge_index[1]
        inv_sqrt_d = jnp.float32(1.0 / np.sqrt(D))
        score = Kh[src] * Qh[dst] * inv_sqrt_d * Eh
        score = jnp.exp(jnp.clip(score.sum(-1, keepdims=True), -5.0, 5.0))
        msg = Vh[src] * score
        wV = jax.ops.segment_sum(msg, dst, num_segments=n)
        return wV.reshape(n, H * D)
    edge_index = jnp.stack([src, dst])
    h = jnp.maximum(_layernorm(x, axis=-1), 0.0)
    x = x + _L0_gnn_ref(h, edge_index, L0_gnn_W1, L0_gnn_b1, L0_gnn_W2, L0_gnn_b2, L0_gnn_W3, L0_gnn_b3, L0_gnn_W4, L0_gnn_b4)
    h = jnp.maximum(_layernorm(x, axis=-1), 0.0)
    x = x + _L1_gnn_ref(h, edge_attr_32, src, dst, L1_gnn_W1, L1_gnn_b1, L1_gnn_W2, L1_gnn_b2, L1_gnn_Wa1, L1_gnn_ba1, L1_gnn_Wa2, L1_gnn_ba2, L1_gnn_Wu1, L1_gnn_bu1, L1_gnn_Wu2, L1_gnn_bu2)
    h = jnp.maximum(_layernorm(x, axis=-1), 0.0)
    x = x + _L2_gnn_ref(h, src, dst, L2_gnn_W, L2_gnn_b)
    h = jnp.maximum(_layernorm(x, axis=-1), 0.0)
    x = x + _L3_gnn_ref(h, edge_attr_64, edge_index, L3_gnn_WQ, L3_gnn_bQ, L3_gnn_WK, L3_gnn_bK, L3_gnn_WE, L3_gnn_bE, L3_gnn_WV, L3_gnn_bV)
    return x

_drawn_inputs = setup_inputs


def setup_inputs(seed=0):
    import zlib

    import numpy as np

    out = dict(_drawn_inputs(seed))
    spreads = {'L0_gnn_b1': (0.0, 0.1),
     'L0_gnn_b2': (0.0, 0.1),
     'L0_gnn_b3': (0.0, 0.1),
     'L0_gnn_b4': (0.0, 0.1),
     'L1_gnn_b1': (0.0, 0.8),
     'L1_gnn_b2': (0.0, 0.8),
     'L1_gnn_ba1': (0.0, 0.8),
     'L1_gnn_bu1': (0.0, 0.1),
     'L1_gnn_bu2': (0.0, 0.1)}
    factors = {'edge_attr_32': 8.0,
     'L1_gnn_W1': 8.0,
     'L1_gnn_W2': 8.0,
     'L1_gnn_Wa1': 8.0,
     'L1_gnn_Wa2': 8.0,
     'L3_gnn_bQ': 8.0,
     'L3_gnn_bK': 8.0,
     'L3_gnn_bE': 8.0}
    for name, (base, spread) in spreads.items():
        noise = np.random.default_rng([zlib.crc32(name.encode()), seed]).standard_normal(out[name].shape)
        drawn = base * np.exp(spread * noise) if base else spread * noise
        out[name] = jnp.asarray(drawn.astype(out[name].dtype))
    for name, factor in factors.items():
        out[name] = (out[name] * factor).astype(out[name].dtype)
    return out
```

```python
import concourse.bass as bass
from concourse import mybir
from contextlib import ExitStack
from collections import namedtuple

F32 = mybir.dt.float32
BF16 = mybir.dt.bfloat16
I32 = mybir.dt.int32
ALU = mybir.AluOpType
ACT = mybir.ActivationFunctionType
AX = mybir.AxisListType

NODES = 12500
EDGES = 200000
P = 128
D = 64
ED1 = 32
HEADS = 8

G = 4
GE = G * P
SLOTS = 4
NG = -(-EDGES // (GE * SLOTS)) * SLOTS
FULL = EDGES // GE
TAIL = EDGES - FULL * GE
REPEATED = (GE - TAIL) // G
QG = NG // SLOTS
NB = -(-NODES // P)
NBW = NB + 1
LAST = NODES - (NB - 1) * P
CB = 14
CHUNKS = NB // CB
PAIRS = CB // 2
WIN = 2 * P
LAG = 2
NOWHERE = -4096.0
HUGE = 1.0e30
EPS = 1.0e-5
assert NG - FULL == 2 and TAIL % G == 0 and NB % CB == 0 and EDGES % GE == TAIL

PAIR_W = {"L0_gnn_W1": 0, "L0_gnn_W2": 1, "L0_gnn_W3": 2, "L0_gnn_W4": 3, "L1_gnn_W2": 4, "Wu1_node": 5, "Wu1_sum": 6,
          "L1_gnn_Wu2": 7, "L3_gnn_WQ": 8, "L3_gnn_WE": 9}
WIDE_W = {"sender": 0, "receiver": 1, "key_value": 2}
VECTORS = {"L0_gnn_b1": 0, "L0_gnn_b2": 1, "L0_gnn_b3": 2, "L0_gnn_b4": 3, "L1_gnn_b1": 4, "L1_gnn_ba1": 5, "L1_gnn_b2": 6,
           "L1_gnn_bu1": 7, "L1_gnn_bu2": 8, "L1_gnn_Wa2": 9, "L2_source": 10, "L2_dest": 11, "L3_gnn_bK": 12,
           "L3_gnn_bV": 13, "L3_gnn_bQ": 14, "L3_gnn_bE": 15}

Step = namedtuple("Step", "n group window slot par fill back")


def gnn_program(nc, src, dst, io, layers=(0, 1, 2, 3)):
    ctx = ExitStack()
    with ctx:
        def sb(name, shape, dt=F32):
            return ctx.enter_context(nc.sbuf_tensor("sb_" + name, shape, dt))

        def sem(name):
            return ctx.enter_context(nc.semaphore(name))

        x = sb("x", [P, NB, D])
        h = sb("h", [P, NB, D])
        acc = sb("acc", [P, NBW, D + 1])
        big = sb("big", [P, NBW, 2 * D])
        dis = sb("dis", [P, NB])
        dst_at = sb("dst_at", [P, NG, G])
        row_at = sb("row_at", [P, NG, G], I32)
        win_row = sb("win_row", [1, 2, NG + 8], I32)
        more = sb("more", [1, 8], I32)
        row_now = sb("row_now", [P, SLOTS, G], I32)
        rows = sb("rows", [P, SLOTS, G, 2 * D])
        feats = sb("feats", [P, SLOTS, G, D])
        onehot = sb("onehot", [P, SLOTS, G, WIN])
        onehot_t = sb("onehot_t", [P, 2, 2, G * P])
        work = sb("work", [P, 2, CB * D])
        hc = sb("hc", [P, CB * D])
        ht = sb("ht", [P, CB * D])
        iota = sb("iota", [P, WIN])
        iota16 = sb("iota16", [P, P], BF16)
        minus_block = sb("minus_block", [P, NBW])
        plus_block = sb("plus_block", [P, NBW])
        past_window = sb("past_window", [P, NBW])
        ident = sb("ident", [P, P])
        zeros16 = sb("zeros16", [P, P], BF16)
        ones = sb("ones", [P, P])
        pair_w = sb("pair_w", [P, len(PAIR_W), 2, D])
        wide_w = sb("wide_w", [P, len(WIDE_W), 2, 2 * D])
        edge_w = sb("edge_w", [P, G, 2 * D])
        stat = sb("stat", [P, 3, CB])
        vectors = sb("vectors", [P, len(VECTORS), D])
        consts = sb("consts", [P, 2])
        psum = [ctx.enter_context(nc.psum_tensor(f"bank{i}", [P, 512], F32)) for i in range(8)]

        tables = [nc.dram_tensor(f"table{i}", [P, NB, w], F32, kind="Internal").ap()
                  for i, w in enumerate([D, D, D, D, 2 * D, D + 2, 2 * D])]

        raw = big[:, :, :].rearrange("p b f -> p (b f)")
        raw_dst = raw[0:QG, 0:SLOTS * GE].bitcast(I32).rearrange("p (q e) -> p q e", e=GE)
        raw_src = raw[0:QG, SLOTS * GE:2 * SLOTS * GE].bitcast(I32).rearrange("p (q e) -> p q e", e=GE)
        part = raw[0:QG, 2 * SLOTS * GE:3 * SLOTS * GE].bitcast(I32).rearrange("p (q e) -> p q e", e=GE)
        flat = h[:, :, :].rearrange("p b f -> p (b f)")
        hi_f = flat[0:QG, 0:2048].rearrange("p (q e) -> p q e", e=GE)
        lo_f = flat[0:QG, 2048:4096].rearrange("p (q e) -> p q e", e=GE)
        row_f = flat[0:QG, 4096:6144].rearrange("p (q e) -> p q e", e=GE)
        assert SLOTS * GE == 2048
        acc_flat = acc[:, :, :].rearrange("p b f -> p (b f)")
        hi_at = acc_flat[:, 0:NG * G].rearrange("p (g j) -> p g j", j=G)
        lo_at = acc_flat[:, NG * G:2 * NG * G].rearrange("p (g j) -> p g j", j=G)
        hilo16 = acc_flat[:, 2 * NG * G:3 * NG * G].bitcast(BF16).rearrange("p (t g j) -> p t g j", t=2, j=G)
        oh16 = onehot[:, :, :, :].rearrange("p a g w -> p a (g w)").bitcast(BF16)
        lim = stat[0:QG, 0:2, 0:SLOTS]

        s_raw = sem("s_raw")
        s_x = sem("s_x")
        s_x0 = sem("s_x0")
        s_const = sem("s_const")
        s_constf = sem("s_constf")
        s_prep = sem("s_prep")
        s_split = sem("s_split")
        s_quarter = sem("s_quarter")
        s_kept = sem("s_kept")
        s_lim = sem("s_lim")
        s_limrow = sem("s_limrow")
        s_index = sem("s_index")
        s_oh16 = sem("s_oh16")
        s_counted = sem("s_counted")
        s_deg = sem("s_deg")
        s_degrees = sem("s_degrees")
        s_dis = sem("s_dis")
        s_out = sem("s_out")

        def quarter_loads(eng, of, to):
            for q in range(SLOTS - 1):
                at = q * QG * GE
                eng.dma_start(to[:, q, :], of[at:at + QG * GE].rearrange("(g e) -> g e", e=GE)).then_inc(s_raw, 16)
            at = (SLOTS - 1) * QG * GE
            left = FULL - (SLOTS - 1) * QG
            eng.dma_start(to[0:left, SLOTS - 1, :], of[at:at + left * GE].rearrange("(g e) -> g e", e=GE)).then_inc(s_raw, 16)
            for g in range(left, QG):
                eng.dma_start(to[g:g + 1, SLOTS - 1, :], of[EDGES - GE:EDGES].rearrange("(g e) -> g e", e=GE)).then_inc(s_raw, 16)

        RAW_LOADS = 2 * (SLOTS + QG - (FULL - (SLOTS - 1) * QG))

        def prep_sync(sp):
            quarter_loads(sp, dst, raw_dst)
            quarter_loads(sp, src, raw_src)
            sp.dma_start(x[:, 0:NB - 1, :], io["x"][0:(NB - 1) * P, :].rearrange("(b p) c -> p b c", p=P)).then_inc(s_x, 16)
            sp.wait_ge(s_x0, 1)
            sp.dma_start(x[0:LAST, NB - 1, :], io["x"][(NB - 1) * P:NODES, :]).then_inc(s_x, 16)

        def prep_pool(pool):
            nc.gpsimd.memset(ident[:, :], 0.0).then_inc(s_const, 1)
            nc.gpsimd.memset(zeros16[:, :], 0.0).then_inc(s_const, 1)
            nc.gpsimd.iota(iota[:, :], pattern=[[1, WIN]], base=0, channel_multiplier=0,
                           allow_small_or_imprecise_dtypes=True).then_inc(s_const, 1)
            nc.gpsimd.iota(minus_block[:, :], pattern=[[-P, NBW]], base=0, channel_multiplier=0,
                           allow_small_or_imprecise_dtypes=True).then_inc(s_const, 1)
            nc.gpsimd.iota(plus_block[:, :], pattern=[[P, NBW]], base=0, channel_multiplier=0,
                           allow_small_or_imprecise_dtypes=True).then_inc(s_const, 1)
            nc.gpsimd.iota(past_window[:, :], pattern=[[-P, NBW]], base=1 - WIN, channel_multiplier=0,
                           allow_small_or_imprecise_dtypes=True).then_inc(s_const, 1)
            pool.wait_ge(s_const, 6)
            nc.gpsimd.tensor_copy(iota16[:, :], iota[:, 0:P]).then_inc(s_const, 1)
            nc.gpsimd.affine_select(out=ident[:, :], in_=ident[:, :], compare_op=ALU.not_equal, fill=1.0, base=0,
                                    pattern=[[-1, P]], channel_multiplier=1).then_inc(s_const, 1)

        CONSTS = 8

        class Link:
            def __init__(self, eng, s, base=0):
                self.eng, self.s, self.base, self.k = eng, s, base, 0

            def __call__(self, ins):
                ins.then_inc(self.s, 1)
                self.k += 1
                self.eng.wait_ge(self.s, self.base + self.k)

        def prep_vector(dve):
            nc.vector.memset(x[:, NB - 1, :], 0.0).then_inc(s_x0, 1)
            link = Link(dve, s_prep)
            dve.wait_ge(s_raw, 16 * RAW_LOADS)
            link(nc.vector.tensor_scalar(part, raw_dst, 7, None, ALU.arith_shift_right))
            link(nc.vector.tensor_copy(hi_f, part))
            link(nc.vector.tensor_scalar(part, raw_dst, P - 1, None, ALU.bitwise_and))
            nc.vector.tensor_copy(lo_f, part).then_inc(s_split, 1)
            nc.vector.tensor_reduce(lim[:, 0, :], hi_f, AX.X, ALU.min)
            nc.vector.tensor_reduce(lim[:, 1, :], hi_f, AX.X, ALU.max).then_inc(s_lim, 1)
            dve.wait_ge(s_split, 1)
            link(nc.vector.tensor_scalar(part, raw_src, P - 1, None, ALU.bitwise_and))
            link(nc.vector.tensor_scalar(row_f, part, float(NB), None, ALU.mult))
            link(nc.vector.tensor_scalar(part, raw_src, 7, None, ALU.arith_shift_right))
            nc.vector.tensor_tensor(row_f, row_f, part, ALU.add).then_inc(s_split, 1)
            k = 0
            for to in (hi_at, lo_at, row_at):
                for q in range(SLOTS):
                    k += 1
                    dve.wait_ge(s_quarter, k)
                    bank = psum[k % 2][:, 0:G * QG].rearrange("p (j g) -> p g j", g=QG)
                    nc.vector.tensor_copy(to[:, q * QG:(q + 1) * QG, :], bank).then_inc(s_kept, 1)
            dve.wait_ge(s_kept, k)
            link(nc.vector.scalar_tensor_tensor(dst_at[:, :, :], hi_at, float(P), lo_at, ALU.mult, ALU.add))
            link(nc.vector.memset(dst_at[0:REPEATED, FULL, :], NOWHERE))
            link(nc.vector.memset(dst_at[:, FULL + 1, :], NOWHERE))
            for at in (hi_at, lo_at):
                link(nc.vector.memset(at[0:REPEATED, FULL, :], -1.0))
                link(nc.vector.memset(at[:, FULL + 1, :], -1.0))
            link(nc.vector.tensor_copy(hilo16[:, 0], hi_at))
            link(nc.vector.tensor_copy(hilo16[:, 1], lo_at))
            dve.wait_ge(s_limrow, 1)
            link(nc.vector.memset(win_row[:, :, :], 0))
            link(nc.vector.tensor_copy(win_row[:, 0, 0:NG], psum[2][0:1, 0:NG]))
            link(nc.vector.tensor_copy(win_row[:, 1, 0:NG], psum[3][0:1, 0:NG]))
            reach = hc[0:1, 0:NG]
            link(nc.vector.tensor_copy(reach, psum[2][0:1, 0:NG]))
            link(nc.vector.tensor_tensor(reach, psum[3][0:1, 0:NG], reach, ALU.subtract))
            link(nc.vector.tensor_reduce(hc[0:1, NG:NG + 1], reach, AX.X, ALU.max))
            link(nc.vector.tensor_scalar(more[0:1, 0:1], hc[0:1, NG:NG + 1], -1.0, None, ALU.add))
            dve.sem_inc(s_index, 1)
            with dve.Fori(0, NG // 2) as i:
                for u in range(2):
                    dve.wait_ge(s_counted, 2 * i + u + 1)
                    g = 2 * i + u
                    buf = oh16[:, u]
                    nc.vector.tensor_tensor(
                        buf[:, 0:G * P].rearrange("p (j w) -> p j w", w=P),
                        hilo16[:, 1, bass.ds(g, 1), :].rearrange("p g j -> p (g j)")[:, :, None].to_broadcast([P, G, P]),
                        iota16[:, None, :].to_broadcast([P, G, P]), ALU.is_equal)
                    nc.vector.tensor_tensor(
                        buf[:, G * P:G * (P + NB)].rearrange("p (j w) -> p j w", w=NB),
                        hilo16[:, 0, bass.ds(g, 1), :].rearrange("p g j -> p (g j)")[:, :, None].to_broadcast([P, G, NB]),
                        iota16[:, None, 0:NB].to_broadcast([P, G, NB]), ALU.is_equal).then_inc(s_oh16, 1)
            dve.wait_ge(s_deg, 1)
            link(nc.vector.tensor_scalar(dis[:, :], psum[4][:, 0:NB], 1.0, 1.0, ALU.add, ALU.max))
            dve.sem_inc(s_degrees, 1)
            dve.wait_ge(s_dis, 1)
            link(nc.vector.reciprocal(dis[:, :], dis[:, :]))
            link(nc.vector.memset(acc[:, :, :], 0.0))

        def prep_tensor(pe):
            pe.wait_ge(s_const, CONSTS)
            k = 0
            for of in (hi_f, lo_f, row_f):
                pe.wait_ge(s_split, 2 if of is row_f else 1)
                for q in range(SLOTS):
                    k += 1
                    if k > 2:
                        pe.wait_ge(s_kept, k - 2)
                    for j in range(G):
                        mm = nc.tensor.transpose(psum[k % 2][:, j * QG:(j + 1) * QG], of[:, q, j:GE:G], ident[0:QG, 0:QG])
                    mm.then_inc(s_quarter, 1)
            pe.wait_ge(s_lim, 1)
            for t in range(2):
                for q in range(SLOTS):
                    mm = nc.tensor.matmul(psum[2 + t][0:1, q * QG:(q + 1) * QG], lim[:, t, q:q + 1], ident[0:QG, 0:QG],
                                          start=True, stop=True)
            mm.then_inc(s_limrow, 1)
            pe.sem_inc(s_counted, 2)
            nc.tensor.matmul(psum[4][:, 0:NB], zeros16[:, :], zeros16[:, 0:NB], start=True, stop=False, skip_group_check=True)
            with pe.Fori(0, NG // 2) as i:
                for u in range(2):
                    pe.wait_ge(s_oh16, 2 * i + u + 1)
                    for j in range(G):
                        mm = nc.tensor.matmul(psum[4][:, 0:NB], oh16[:, u, j * P:(j + 1) * P],
                                              oh16[:, u, G * P + j * NB:G * P + (j + 1) * NB], start=False, stop=False,
                                              skip_group_check=True)
                    mm.then_inc(s_counted, 1)
            nc.tensor.matmul(psum[4][:, 0:NB], zeros16[:, :], zeros16[:, 0:NB], start=False, stop=True,
                             skip_group_check=True).then_inc(s_deg, 1)

        s_spare = sem("s_spare")

        def take_waits(eng):
            eng.sem_inc(s_spare, 1)

        named = [0]

        def register(eng, name):
            named[0] += 1
            return eng.alloc_register(f"{name}{named[0]}")

        def edge_pass(eng, stages, serial=None):
            deepest = max(0, *(lag for _, lag in stages))
            ahead = -min(0, min(lag for _, lag in stages))
            assert ahead in (0, SLOTS) and deepest <= SLOTS
            steady = NG // SLOTS - ahead // SLOTS
            regs = [register(eng, "window") for i in range(SLOTS + deepest)]

            def moment(t, u, i, windows):
                for stage, lag in stages:
                    if t is not None and not 0 <= t - lag < NG:
                        continue
                    w = windows[u - lag + deepest] if lag >= 0 else None
                    stage(Step(n=SLOTS * i + u - lag + 1, group=SLOTS * i + u - lag, window=w, slot=(u - lag) % SLOTS,
                               par=(u - lag) % 2, fill=i + 1 + (u - lag) // SLOTS, back=0))

            def load_windows(i):
                if all(lag < 0 for _, lag in stages):
                    return None
                if isinstance(i, int) and i == 0:
                    eng.load(regs[deepest:], win_row[0:1, 0, 0:SLOTS])
                else:
                    eng.load(regs, win_row[0:1, 0, bass.ds(SLOTS * i - deepest, SLOTS + deepest)])
                have = regs[deepest:] if isinstance(i, int) and i == 0 else regs
                return [None] * (len(regs) - len(have)) + [eng.snap(r, min_val=0, max_val=NB - 1) for r in have]

            for t in range(-ahead, 0):
                for stage, lag in stages:
                    if t - lag >= 0:
                        stage(Step(n=t - lag + 1, group=t - lag, window=None, slot=(t - lag) % SLOTS, par=(t - lag) % 2,
                                   fill=1 + (t - lag) // SLOTS, back=0))
            windows = load_windows(0)
            for u in range(SLOTS):
                moment(u, u, 0, windows)
            with eng.Fori(1, steady) as i:
                windows = load_windows(i)
                for u in range(SLOTS):
                    moment(None, u, i, windows)
            for t in range(SLOTS * steady, NG + deepest):
                if t % SLOTS == 0:
                    windows = load_windows(t // SLOTS)
                moment(t, t % SLOTS, t // SLOTS, windows)

            beyond(eng, lambda step: [stage(step) for stage in (serial or [stage for stage, _ in stages])])
            for r in regs:
                eng.free_register(r)

        def beyond(eng, work_on):
            count = register(eng, "count")
            eng.reg_mov(count, 0)
            ends = [register(eng, "first"), register(eng, "last")]
            some = eng.value_load(more[0:1, 0:1], min_val=-1, max_val=NB)
            with eng.If(some > 0):
                with eng.Fori(0, NG) as g:
                    eng.load([ends[0]], win_row[0:1, 0, bass.ds(g, 1)])
                    eng.load([ends[1]], win_row[0:1, 1, bass.ds(g, 1)])
                    first, last = (eng.snap(r, min_val=0, max_val=NB - 1) for r in ends)
                    with eng.If(first + 1 < last):
                        with eng.Fori(first + 2, last + 1, 2) as w:
                            eng.reg_add(count, count, 1)
                            k = eng.snap(count, min_val=1, max_val=NG * NB)
                            work_on(Step(n=NG + k, group=g, window=w, slot=0, par=0, fill=NG // SLOTS + k, back=1))
                    eng.reg_mov(ends[0], 0)
                eng.reg_mov(ends[0], 0)
            eng.free_register(count)
            for r in ends:
                eng.free_register(r)

        def dst_of(g):
            return dst_at[:, bass.ds(g, 1), :].rearrange("p g j -> p (g j)")

        def build_onehot(step):
            return nc.vector.scalar_tensor_tensor(
                onehot[:, step.slot], dst_of(step.group)[:, :, None].to_broadcast([P, G, WIN]),
                minus_block[:, bass.ds(step.window, 1)], iota[:, None, :].to_broadcast([P, G, WIN]), ALU.add, ALU.is_equal)

        def gather_pass(pool, table, width, s_rows, s_free, s_staged):
            view = table.rearrange("p b f -> (p b) f")

            def fetch(slot, n, back=0):
                n, used = pool.snap(n), pool.snap(n + back)
                pool.wait_ge(s_free, used)
                pool.wait_ge(s_staged, n)
                take_waits(pool)
                for j in range(G):
                    nc.gpsimd.indirect_dma_start(
                        out=rows[:, slot, j, 0:width], out_offset=None, in_=view,
                        in_offset=bass.IndirectOffsetOnAxis(ap=row_now[:, slot, j:j + 1], axis=0),
                        bounds_check=P * NB - 1).then_inc(s_rows[slot], 16)

            with pool.Fori(0, NG // SLOTS) as i:
                for u in range(SLOTS):
                    fetch(u, SLOTS * i + u + 1)
            beyond(pool, lambda step: fetch(0, step.n, SLOTS - 1))

        def stage_rows(act, s_rows, s_staged):
            def stage(step):
                if not (isinstance(step.fill, int) and step.fill == 1):
                    act.wait_ge(s_rows[step.slot], 16 * G * (step.fill - 1))
                take_waits(act)
                at = row_at[:, bass.ds(step.group, 1), :].rearrange("p g j -> p (g j)")
                nc.scalar.activation(row_now[:, step.slot, :], at, ACT.Copy).then_inc(s_staged, 1)

            return stage

        s_w0, s_w = sem("s_w0"), sem("s_w")
        s_var = sem("s_var")
        s_rstd = sem("s_rstd")
        NORM_LINKS = 7

        def weight_loads(sp):
            sp.wait_ge(s_w0, 3)
            n = 0

            def load(to, of):
                nonlocal n
                sp.dma_start(to, of).then_inc(s_w, 16)
                n += 1

            u1 = io["L1_gnn_Wu1"]
            for name, at in PAIR_W.items():
                w = {"Wu1_node": u1[0:D, :], "Wu1_sum": u1[D:2 * D, :]}.get(name, io[name] if name in io else None)
                for half in range(2):
                    load(pair_w[D * half:D * half + D, at, half, :], w)
            for half in range(2):
                rows_of = slice(D * half, D * half + D)
                for part, name in enumerate(("L1_gnn_W1", "L1_gnn_Wa1")):
                    cols = slice(D * part, D * part + D)
                    load(wide_w[rows_of, WIDE_W["sender"], half, cols], io[name][0:D, :])
                    load(wide_w[rows_of, WIDE_W["receiver"], half, cols], io[name][D:2 * D, :])
                for part, name in enumerate(("L3_gnn_WK", "L3_gnn_WV")):
                    load(wide_w[rows_of, WIDE_W["key_value"], half, D * part:D * part + D], io[name])
            for j in range(G):
                for part, name in enumerate(("L1_gnn_W1", "L1_gnn_Wa1")):
                    load(edge_w[ED1 * j:ED1 * j + ED1, j, D * part:D * part + D], io[name][2 * D:2 * D + ED1, :])
            for name, at in VECTORS.items():
                if name == "L2_source":
                    v = io["L2_gnn_W"][0:1, 0:D]
                elif name == "L2_dest":
                    v = io["L2_gnn_W"][0:1, D:2 * D]
                elif name == "L1_gnn_Wa2":
                    v = io[name].rearrange("f a -> a f")
                else:
                    v = io[name].rearrange("(a f) -> a f", a=1)
                load(vectors[:, at, :], v.to_broadcast([P, D]))
            load(consts[:, 0:1], io["L2_gnn_b"].rearrange("(a f) -> a f", a=1).to_broadcast([P, 1]))
            load(consts[:, 1:2], io["L1_gnn_ba2"].rearrange("(a f) -> a f", a=1).to_broadcast([P, 1]))
            assert n == WEIGHT_LOADS

        WEIGHT_LOADS = 2 * len(PAIR_W) + 12 + 2 * G + len(VECTORS) + 2

        def chunk(t, c, width=D):
            return t[:, bass.ds(CB * c, CB), 0:width]

        def v3(t, f=D):
            return t.rearrange("p (b f) -> p b f", f=f)

        def vector_of(name, n, width=1):
            at = VECTORS[name]
            return vectors[:, at:at + width, :].rearrange("p a f -> p (a f)")[:, None, :].to_broadcast([P, n, width * D])

        def relu_layernorm(dve, link, c, before):
            xc = chunk(x, c)
            mean, var, rstd = stat[:, 0, :], stat[:, 1, :], stat[:, 2, :]
            link(nc.vector.tensor_reduce(mean, xc, AX.X, ALU.add))
            link(nc.vector.scalar_tensor_tensor(v3(work[:, 0, :]), mean[:, :, None].to_broadcast([P, CB, D]), -1.0 / D, xc,
                                                ALU.mult, ALU.add))
            link(nc.vector.tensor_tensor(work[:, 1, :], work[:, 0, :], work[:, 0, :], ALU.mult))
            link(nc.vector.tensor_reduce(var, v3(work[:, 1, :]), AX.X, ALU.add))
            link(nc.vector.tensor_scalar(var, var, 1.0 / D, EPS, ALU.mult, ALU.add))
            dve.sem_inc(s_var, 1)
            dve.wait_ge(s_rstd, c + before + 1)
            link(nc.vector.reciprocal(rstd, rstd))
            link(nc.vector.scalar_tensor_tensor(v3(hc[:, :]), v3(work[:, 0, :]), 0.0, rstd[:, :, None].to_broadcast([P, CB, D]),
                                                ALU.max, ALU.mult))

        def root_of_var(act, c, before):
            act.wait_ge(s_var, c + before + 1)
            nc.scalar.activation(stat[:, 2, :], stat[:, 1, :], ACT.Sqrt).then_inc(s_rstd, 1)

        def dis_of(c):
            return dis[:, bass.ds(CB * c, CB)][:, :, None].to_broadcast([P, CB, D])

        def turn_pairs(of):
            for p in range(PAIRS):
                mm = nc.tensor.transpose(psum[p // 4][:, (p % 4) * P:(p % 4 + 1) * P], of[:, p * P:(p + 1) * P], ident[:, :])
            return mm

        def copy_turned(fn=ACT.Copy):
            nc.scalar.activation(ht[:, 0:512], psum[0][:, :], fn)
            return nc.scalar.activation(ht[:, 512:CB * D], psum[1][:, 0:CB * D - 512], fn)

        def times_pairs(w, start=True, stop=True, of=ht):
            for p in range(PAIRS):
                mm = nc.tensor.matmul(psum[2 + p // 4][:, (p % 4) * P:(p % 4 + 1) * P], of[:, p * P:(p + 1) * P],
                                      pair_w[:, PAIR_W[w], :, :], start=start and p % 4 == 0, stop=stop, skip_group_check=True)
            return mm

        def times_wide(w):
            for p in range(PAIRS):
                mm = nc.tensor.matmul(psum[2 + p // 2][:, (p % 2) * WIN:(p % 2 + 1) * WIN], ht[:, p * P:(p + 1) * P],
                                      wide_w[:, WIDE_W[w], :, :], start=True, stop=True)
            return mm

        NARROW = [(2, 0, 8), (3, 8, CB - 8)]
        WIDE = [(2, 0, 4), (3, 4, 4), (4, 8, 4), (5, 12, 2)]

        s_hc, s_turned, s_ht = sem("s_hc"), sem("s_turned"), sem("s_ht")
        s_conv_link, s_conv_product = sem("s_conv_link"), sem("s_conv_product")
        s_conv_made, s_conv_table = sem("s_conv_made"), sem("s_conv_table")

        class Pass:
            def __init__(self, n, at=0):
                self.at = at
                self.s_rows = [sem(n + f"rows{i}") for i in range(SLOTS)]
                self.s_staged = sem(n + "staged")
                self.s_onehot = sem(n + "onehot")
                self.s_summed = sem(n + "summed")
                self.s_added = sem(n + "added")

        class Layer(Pass):
            def __init__(self, n, at=0):
                super().__init__(n, at)
                self.s_link, self.s_acc = sem(n + "link"), sem(n + "acc")
                self.s_made = sem(n + "made")
                self.s_table = sem(n + "table")
                self.s_slink, self.s_plink = sem(n + "slink"), sem(n + "plink")
                self.s_onehot_turned = sem(n + "oht")
                self.s_turned_copied = sem(n + "ohc")
                self.s_message = sem(n + "mes")

        def write_table(sp, s_made, s_table, table, of, at=0):
            with sp.Fori(0, CHUNKS) as c:
                sp.wait_ge(s_made, c + at + 1)
                sp.dma_start(table[:, bass.ds(CB * c, CB), :], of(c)).then_inc(s_table, 16)

        def sum_edges(pe, s, step, message, width):
            pe.wait_ge(s.s_added, step.n + step.back)
            for c in range(2):
                for j in range(G):
                    mm = nc.tensor.matmul(psum[4 + step.par][:, c * width:(c + 1) * width],
                                          onehot[:, step.slot, j, c * P:(c + 1) * P], message(j),
                                          start=(j == 0), stop=(j == G - 1), skip_group_check=True)
            mm.then_inc(s.s_summed, 1)

        def onehot_stage(dve, s):
            def stage(step):
                dve.wait_ge(s.s_summed, step.n + step.back * (SLOTS - 1))
                build_onehot(step).then_inc(s.s_onehot, 1)

            return stage

        def conv_vector(dve, k, s):
            LINKS = NORM_LINKS if k == 0 else 2
            with dve.Fori(0, CHUNKS) as c:
                dve.wait_ge(s_turned, c + s.at + 1)
                link = Link(dve, s_conv_link, c * LINKS + (CHUNKS * (NORM_LINKS + 2 * (k - 1)) if k else 0))
                if k == 0:
                    relu_layernorm(dve, link, c, 0)
                else:
                    link(nc.vector.tensor_tensor(v3(hc[:, :]), chunk(acc, c), dis_of(c), ALU.mult))
                    link(nc.vector.tensor_tensor(v3(hc[:, :]), v3(hc[:, :]), vector_of(f"L0_gnn_b{k}", CB), ALU.add))
                dve.sem_inc(s_hc, 1)
                dve.wait_ge(s_conv_product, c + s.at + 1)
                for bank, b, n in NARROW:
                    ins = nc.vector.tensor_tensor(acc[:, bass.ds(CB * c + b, n), 0:D], v3(psum[bank][:, 0:n * D]),
                                                  dis[:, bass.ds(CB * c + b, n)][:, :, None].to_broadcast([P, n, D]), ALU.mult)
                ins.then_inc(s_conv_made, 1)
            dve.wait_ge(s_conv_made, s.at + CHUNKS)
            dve.sem_inc(s.s_summed, SLOTS)
            dve.sem_inc(s.s_added, 2)
            dve.wait_ge(s_conv_table, 16 * (s.at + CHUNKS))

            def add_sums(step):
                dve.wait_ge(s.s_summed, step.n + SLOTS)
                dve.wait_ge(s.s_added, step.n + 1)
                to = acc[:, bass.ds(step.window, 2), 0:D]
                nc.vector.tensor_tensor(to, to, v3(psum[4 + step.par][:, 0:2 * D]), ALU.add).then_inc(s.s_added, 1)

            edge_pass(dve, [(onehot_stage(dve, s), 0), (add_sums, 2)])

        def conv_scalar(act, k, s):
            if k == 0:
                act.wait_ge(s_degrees, 1)
                nc.scalar.activation(dis[:, :], dis[:, :], ACT.Sqrt).then_inc(s_dis, 1)
            with act.Fori(0, CHUNKS) as c:
                if k == 0:
                    root_of_var(act, c, 0)
                act.wait_ge(s_turned, c + s.at + 2)
                copy_turned(ACT.Relu).then_inc(s_ht, 1)
            edge_pass(act, [(stage_rows(act, s.s_rows, s.s_staged), -SLOTS)])

        def conv_tensor(pe, k, s):
            with pe.Fori(0, CHUNKS) as c:
                pe.wait_ge(s_hc, c + s.at + 1)
                turn_pairs(hc).then_inc(s_turned, 1)
                pe.wait_ge(s_ht, c + s.at + 1)
                times_pairs(f"L0_gnn_W{k + 1}").then_inc(s_conv_product, 1)

            def sums(step):
                pe.wait_ge(s.s_onehot, step.n)
                pe.wait_ge(s.s_rows[step.slot], 16 * G * step.fill)
                sum_edges(pe, s, step, lambda j: rows[:, step.slot, j, 0:D], D)

            edge_pass(pe, [(sums, 0)])

        def conv_end_vector(dve):
            with dve.Fori(0, CHUNKS) as c:
                link = Link(dve, s_conv_link, c * 3 + CHUNKS * (NORM_LINKS + 6))
                link(nc.vector.tensor_tensor(v3(hc[:, :]), chunk(acc, c), dis_of(c), ALU.mult))
                link(nc.vector.tensor_tensor(v3(hc[:, :]), v3(hc[:, :]), vector_of("L0_gnn_b4", CB), ALU.add))
                link(nc.vector.tensor_tensor(chunk(x, c), chunk(x, c), v3(hc[:, :]), ALU.add))


        def load_features(sp, attrs, s_feats, s_used):
            f = attrs.shape[1]

            def load(at, slot, n, back=0):
                sp.wait_ge(s_used, n + back)
                sp.dma_start(feats[:, slot, :, :].rearrange("p j f -> p (j f)")[:, 0:G * f],
                             attrs[bass.ds(at, GE), :].rearrange("(p j) f -> p (j f)", j=G)).then_inc(s_feats[slot], 16)

            with sp.Fori(0, FULL // SLOTS) as i:
                for u in range(SLOTS):
                    load((SLOTS * i + u) * GE, u, SLOTS * i + u + 1)
            for g in range(FULL // SLOTS * SLOTS, NG):
                load(g * GE if g < FULL else EDGES - GE, g % SLOTS, g + 1)

            def again(step):
                n = sp.snap(step.n)
                with sp.If(step.group < FULL):
                    load(step.group.with_bounds(min_val=0, max_val=FULL - 1) * GE, 0, n, SLOTS - 1)
                with sp.If(step.group > FULL - 1):
                    load(EDGES - GE, 0, n, SLOTS - 1)
                take_waits(sp)

            beyond(sp, again)

        scratch = work[:, :, :].rearrange("p a f -> p (a f)")
        pre = [scratch[:, 0:512], scratch[:, 512:1024]]
        message = [hc[:, i * G * (D + 1):(i + 1) * G * (D + 1)].rearrange("p (j f) -> p j f", f=D + 1) for i in range(2)]
        swish = ht[:, 0:512]
        product = scratch[:, 1024:1280]
        feats_t = [scratch[:, 1280:1536], scratch[:, 1536:1792]]
        tiny = hc[:, 2 * G * (D + 1):2 * G * (D + 1) + 256]
        assert 2 * G * (D + 1) + 256 <= CB * D

        def turn_onehot(pe, s, step):
            pe.wait_ge(s.s_onehot, step.n)
            pe.wait_ge(s.s_turned_copied, step.n)
            for c in range(2):
                for j in range(G):
                    mm = nc.tensor.transpose(psum[c][:, j * P:(j + 1) * P], onehot[:, step.slot, j, c * P:(c + 1) * P],
                                             ident[:, :])
            return mm

        def add_scaled(dve, s, step, coef, width):
            dve.wait_ge(s.s_summed, step.n + SLOTS)
            dve.wait_ge(s.s_added, step.n + 1)
            for c in range(2):
                to = acc[:, bass.ds(step.window + c, 1), 0:width].rearrange("p b f -> p (b f)")
                ins = nc.vector.scalar_tensor_tensor(to, to, coef[:, c:c + 1], psum[4 + step.par][:, c * width:(c + 1) * width],
                                                     ALU.mult, ALU.add)
            ins.then_inc(s.s_added, 1)

        class Messages(Layer):
            def __init__(self, n, at=0):
                super().__init__(n, at)
                self.s_product = sem(n + "product")
                self.s_kept, self.s_read = sem(n + "kept"), sem(n + "read")
                self.s_feats = [sem(n + f"feats{i}") for i in range(SLOTS)]
                self.s_feats_turned = sem(n + "ft")
                self.s_feats_copied = sem(n + "fc")
                self.s_projected = sem(n + "pro")
                self.s_rows_used = sem(n + "use")
                self.s_tanh = sem(n + "tanh")
                self.s_side = sem(n + "side")
                self.s_logits = sem(n + "log")
                self.s_top_turned = sem(n + "tt")
                self.s_top = sem(n + "top")
                self.s_top_spread = sem(n + "ts")
                self.s_weighted = sem(n + "wei")
                self.s_upd_dve, self.s_upd_pe, self.s_upd_act = sem(n + "ud"), sem(n + "up"), sem(n + "ua")
                self.s_sum, self.s_last, self.s_act_link = sem(n + "sum"), sem(n + "last"), sem(n + "alink")

        def messages():
            s = Messages("msg_", CHUNKS * (4 * (0 in layers)))
            staging = rows[:, :, :, :].rearrange("p a j f -> p (a j f)")[:, 0:CB * 2 * D]
            logits = [tiny[:, G * i:G * i + G] for i in range(2)]
            peak = [tiny[:, 8 + i:9 + i] for i in range(2)]
            top = tiny[0:1, 10:11]
            minus_top = [tiny[:, 12 + i:13 + i] for i in range(2)]
            coef = [tiny[:, 16 + 2 * i:18 + 2 * i] for i in range(2)]
            below = [tiny[:, 24 + G * i:24 + G * i + G] for i in range(2)]
            above = [tiny[:, 32 + G * i:32 + G * i + G] for i in range(2)]
            row_peak = tiny[0:1, 40:41]
            blocks = tiny[:, 48:48 + NBW]
            total = tiny[:, 160:162]

            def sync(sp):
                write_table(sp, s.s_made, s.s_table, tables[4], lambda c: v3(staging, 2 * D))
                load_features(sp, io["edge_attr_32"], s.s_feats, s.s_feats_turned)

            def gpsimd(pool):
                pool.wait_ge(s.s_table, 16 * (CHUNKS + 1))
                gather_pass(pool, tables[4], 2 * D, s.s_rows, s.s_rows_used, s.s_staged)

            def vector(dve):
                before = norms_before(1)
                dve.sem_inc(s.s_table, 16)
                first = Link(dve, s.s_acc)
                first(nc.vector.memset(acc[:, :, :], 0.0))
                with dve.Fori(0, CHUNKS) as c:
                    dve.wait_ge(s_turned, c + s.at + 1)
                    link = Link(dve, s.s_link, c * (NORM_LINKS + 1))
                    relu_layernorm(dve, link, c, before)
                    dve.sem_inc(s_hc, 1)
                    link(nc.vector.tensor_copy(chunk(h, c), v3(hc[:, :])))
                    dve.wait_ge(s.s_product, 2 * c + 1)
                    for bank, b, n in WIDE:
                        ins = nc.vector.tensor_tensor(big[:, bass.ds(CB * c + b, n), :], v3(psum[bank][:, 0:n * 2 * D], 2 * D),
                                                      vector_of("L1_gnn_b1", n, 2), ALU.add)
                    ins.then_inc(s.s_kept, 1)
                dve.wait_ge(s.s_kept, CHUNKS)
                dve.wait_ge(s.s_table, 16 * (CHUNKS + 1))
                first(nc.vector.memset(blocks, -HUGE))
                first(nc.vector.memset(top, -HUGE))
                for credited, n in ((s.s_summed, SLOTS), (s.s_added, 2), (s.s_turned_copied, 1), (s.s_feats_turned, SLOTS),
                                    (s.s_feats_copied, 1), (s.s_projected, 2), (s.s_rows_used, SLOTS), (s.s_logits, 2),
                                    (s.s_weighted, 2), (s.s_message, 2), (s.s_top_spread, 1)):
                    dve.sem_inc(credited, n)

                def complete(step):
                    dve.wait_ge(s.s_rows[step.slot], 16 * G * step.fill)
                    dve.wait_ge(s.s_projected, step.n + 2)
                    dve.wait_ge(s.s_message, step.n + step.back)
                    nc.vector.tensor_tensor(v3(pre[step.par], 2 * D), rows[:, step.slot, :, :],
                                            v3(psum[2 + step.par][:, :], 2 * D), ALU.add).then_inc(s.s_rows_used, 1)

                def logit(step):
                    dve.wait_ge(s.s_tanh, step.n)
                    dve.wait_ge(s.s_side, step.n)
                    dve.wait_ge(s.s_weighted, step.n + step.back)
                    link = Link(dve, s.s_plink, 6 * (step.n - 1))
                    v = pre[step.par]
                    link(nc.vector.scalar_tensor_tensor(v, swish, 1.0, v, ALU.add, ALU.mult))
                    l = logits[step.par]
                    link(nc.vector.tensor_tensor(v3(product), v3(v, 2 * D)[:, :, D:2 * D],
                                                 vector_of("L1_gnn_Wa2", G), ALU.mult))
                    link(nc.vector.tensor_reduce(l, v3(product), AX.X, ALU.add))
                    link(nc.vector.tensor_scalar(l, l, 0.5, consts[:, 1:2], ALU.mult, ALU.add))
                    link(nc.vector.scalar_tensor_tensor(l, below[step.par], -HUGE, l, ALU.mult, ALU.add))
                    link(nc.vector.scalar_tensor_tensor(l, above[step.par], -HUGE, l, ALU.mult, ALU.add))
                    nc.vector.tensor_reduce(peak[step.par], l, AX.X, ALU.max).then_inc(s.s_logits, 1)

                def raise_top(step):
                    dve.wait_ge(s.s_top_turned, step.n)
                    dve.wait_ge(s.s_top_spread, step.n)
                    link = Link(dve, s.s_slink, 2 * (step.n - 1))
                    link(nc.vector.tensor_reduce(row_peak, psum[7][0:1, 0:P], AX.X, ALU.max))
                    link(nc.vector.tensor_tensor(top, top, row_peak, ALU.max))
                    dve.sem_inc(s.s_top, 1)

                def weigh(step):
                    dve.wait_ge(s.s_weighted, step.n + 2)
                    m = message[step.par]
                    nc.vector.tensor_tensor(m[:, :, 0:D], v3(pre[step.par], 2 * D)[:, :, 0:D],
                                            m[:, :, D:D + 1].to_broadcast([P, G, D]), ALU.mult).then_inc(s.s_message, 1)

                def add_sums(step):
                    add_scaled(dve, s, step, coef[step.par], D + 1)

                make = onehot_stage(dve, s)
                edge_pass(dve, [(weigh, 3), (make, 0), (logit, 2), (complete, 1), (add_sums, 3), (raise_top, 2)],
                          serial=[make, complete, logit, raise_top, weigh, add_sums])

                first(nc.vector.memset(total, 0.0))
                dve.sem_inc(s.s_upd_dve, 1)
                dve.wait_ge(s.s_upd_act, 1)
                final = work[:, 0, 0:NBW]
                per_block = work[:, 1, 0:NBW]
                first(nc.vector.tensor_tensor(per_block, acc[:, :, D:D + 1].rearrange("p b a -> p (b a)"), final, ALU.mult))
                first(nc.vector.tensor_reduce(total[:, 0:1], per_block, AX.X, ALU.add))
                dve.sem_inc(s.s_sum, 1)
                dve.wait_ge(s.s_sum, 2)
                first(nc.vector.reciprocal(total[:, 0:1], psum[7][:, 0:1]))
                first(nc.vector.tensor_scalar(dis[:, :], final[:, 0:NB], total[:, 0:1], None, ALU.mult))
                dve.sem_inc(s.s_sum, 1)
                for w in ("L1_gnn_W2", "L1_gnn_Wu2"):
                    first(nc.vector.tensor_scalar(pair_w[:, PAIR_W[w]], pair_w[:, PAIR_W[w]], 0.5, None, ALU.mult))
                wide, share = work[:, 0, :], stat[:, 0, :]
                with dve.Fori(0, CHUNKS) as c:
                    link = Link(dve, s.s_link, CHUNKS * (NORM_LINKS + 1) + 8 * c)

                    def banks(k, out, more):
                        dve.wait_ge(s.s_upd_pe, UPD_PE * c + k)
                        for bank, b, n in NARROW:
                            ins = nc.vector.tensor_tensor(v3(out)[:, b:b + n, :], v3(psum[bank][:, 0:n * D]), more(b, n), ALU.add)
                        link(ins)

                    link(nc.vector.tensor_tensor(v3(hc[:, :]), chunk(acc, c), dis_of(c), ALU.mult))
                    dve.sem_inc(s.s_upd_dve, 1)
                    link(nc.vector.tensor_tensor(share, acc[:, bass.ds(CB * c, CB), D:D + 1].rearrange("p b a -> p (b a)"),
                                                 dis[:, bass.ds(CB * c, CB)], ALU.mult))
                    link(nc.vector.tensor_tensor(v3(wide), vector_of("L1_gnn_b2", CB), share[:, :, None].to_broadcast([P, CB, D]),
                                                 ALU.mult))
                    banks(2, hc[:, :], lambda b, n: v3(wide)[:, b:b + n, :])
                    dve.sem_inc(s.s_upd_dve, 1)
                    banks(6, wide, lambda b, n: vector_of("L1_gnn_bu1", n))
                    dve.sem_inc(s.s_upd_dve, 1)
                    dve.wait_ge(s.s_upd_act, UPD_ACT * c + 6)
                    link(nc.vector.scalar_tensor_tensor(hc[:, :], work[:, 1, :], 1.0, wide, ALU.add, ALU.mult))
                    dve.sem_inc(s.s_upd_dve, 1)
                    banks(8, wide, lambda b, n: vector_of("L1_gnn_bu2", n))
                    link(nc.vector.tensor_tensor(chunk(x, c), chunk(x, c), v3(wide), ALU.add))

            UPD_PE, UPD_ACT = 8, 6

            def scalar(act):
                before = norms_before(1)
                with act.Fori(0, CHUNKS) as c:
                    root_of_var(act, c, before)
                    act.wait_ge(s_turned, c + s.at + 2)
                    copy_turned().then_inc(s_ht, 1)
                    act.wait_ge(s.s_product, 2 * c + 2)
                    act.wait_ge(s.s_table, 16 * (c + 1))
                    for bank, b, n in WIDE:
                        ins = nc.scalar.activation(staging[:, b * 2 * D:(b + n) * 2 * D], psum[bank][:, 0:n * 2 * D], ACT.Copy)
                    ins.then_inc(s.s_made, 1)
                    act.wait_ge(s.s_made, c + 1)
                    act.sem_inc(s.s_read, 1)

                def copy_onehot(step):
                    act.wait_ge(s.s_onehot_turned, step.n)
                    act.wait_ge(s.s_projected, step.n + step.back)
                    for c in range(2):
                        ins = nc.scalar.activation(onehot_t[:, step.par, c, :], psum[c][:, :], ACT.Copy)
                    ins.then_inc(s.s_turned_copied, 1)

                def copy_feats(step):
                    act.wait_ge(s.s_feats_turned, step.n + SLOTS)
                    nc.scalar.activation(feats_t[step.par][:, 0:P], psum[6][:, 0:P], ACT.Copy).then_inc(s.s_feats_copied, 1)

                def tanhs(step):
                    act.wait_ge(s.s_rows_used, step.n + SLOTS)
                    act.wait_ge(s.s_logits, step.n + 1)
                    nc.scalar.activation(swish[:, :], pre[step.par], ACT.Tanh, scale=0.5).then_inc(s.s_tanh, 1)

                def sides(step):
                    act.wait_ge(s.s_logits, step.n + step.back)
                    take_waits(act)
                    nc.scalar.activation(below[step.par], dst_of(step.group), ACT.Relu, bias=plus_block[:, bass.ds(step.window, 1)],
                                         scale=-1.0)
                    nc.scalar.activation(above[step.par], dst_of(step.group), ACT.Relu,
                                         bias=past_window[:, bass.ds(step.window, 1)]).then_inc(s.s_side, 1)

                def exps(step):
                    act.wait_ge(s.s_top_spread, step.n + 1)
                    act.wait_ge(s.s_added, step.n + step.back)
                    act.wait_ge(s.s_summed, step.n + 2 + step.back)
                    link = Link(act, s.s_act_link, 3 * (step.n - 1))
                    m = minus_top[step.par]
                    link(nc.scalar.activation(m, psum[7][:, P:P + 1], ACT.Copy, scale=-1.0))
                    at = blocks[:, bass.ds(step.window, 2)]
                    take_waits(act)
                    link(nc.scalar.activation(coef[step.par], at, ACT.Exp, bias=m))
                    take_waits(act)
                    link(nc.scalar.activation(at, psum[7][:, P:P + 1].to_broadcast([P, 2]), ACT.Copy))
                    nc.scalar.activation(message[step.par][:, :, D:D + 1].rearrange("p j a -> p (j a)"), logits[step.par], ACT.Exp,
                                         bias=m).then_inc(s.s_weighted, 1)

                stage = stage_rows(act, s.s_rows, s.s_staged)
                edge_pass(act, [(copy_onehot, 0), (copy_feats, 0), (sides, 1), (tanhs, 1), (exps, 2), (stage, -SLOTS)],
                          serial=[stage, copy_onehot, copy_feats, sides, tanhs, exps])
                act.wait_ge(s.s_upd_dve, 1)
                nc.scalar.activation(minus_top[0], psum[7][:, P:P + 1], ACT.Copy, scale=-1.0).then_inc(s.s_last, 1)
                act.wait_ge(s.s_last, 1)
                nc.scalar.activation(work[:, 0, 0:NBW], blocks, ACT.Exp, bias=minus_top[0]).then_inc(s.s_upd_act, 1)
                act.wait_ge(s.s_sum, 3)
                with act.Fori(0, CHUNKS) as c:
                    def pe_event(k):
                        act.wait_ge(s.s_upd_pe, UPD_PE * c + k)

                    act.wait_ge(s.s_upd_dve, 4 * c + 1)
                    nc.scalar.activation(v3(work[:, 1, :]), chunk(h, c), ACT.Copy).then_inc(s.s_upd_act, 1)
                    pe_event(1)
                    copy_turned().then_inc(s.s_upd_act, 1)
                    pe_event(3)
                    copy_turned().then_inc(s.s_upd_act, 1)
                    pe_event(5)
                    copy_turned().then_inc(s.s_upd_act, 1)
                    act.wait_ge(s.s_upd_dve, 4 * c + 4)
                    nc.scalar.activation(work[:, 1, :], work[:, 0, :], ACT.Tanh, scale=0.5).then_inc(s.s_upd_act, 1)
                    pe_event(7)
                    copy_turned().then_inc(s.s_upd_act, 1)

            def tensor(pe):
                pe.sem_inc(s.s_read, 1)
                with pe.Fori(0, CHUNKS) as c:
                    pe.wait_ge(s_hc, c + s.at + 1)
                    turn_pairs(hc).then_inc(s_turned, 1)
                    pe.wait_ge(s_ht, c + s.at + 1)
                    pe.wait_ge(s.s_read, c + 1)
                    times_wide("receiver").then_inc(s.s_product, 1)
                    pe.wait_ge(s.s_kept, c + 1)
                    times_wide("sender").then_inc(s.s_product, 1)

                def turn(step):
                    turn_onehot(pe, s, step).then_inc(s.s_onehot_turned, 1)

                def turn_feats(step):
                    pe.wait_ge(s.s_feats[step.slot], 16 * step.fill)
                    pe.wait_ge(s.s_feats_copied, step.n)
                    nc.tensor.transpose(psum[6][:, 0:P], feats[:, step.slot, :, :].rearrange("p j f -> p (j f)")[:, 0:P],
                                        ident[:, :]).then_inc(s.s_feats_turned, 1)

                def project(step):
                    pe.wait_ge(s.s_turned_copied, step.n + 1)
                    pe.wait_ge(s.s_feats_copied, step.n + 1)
                    pe.wait_ge(s.s_rows_used, step.n + 2 + step.back)
                    bank = psum[2 + step.par]
                    nc.tensor.matmul(bank[:, :], feats_t[step.par][:, 0:P], edge_w[:, :, :], start=True, stop=False,
                                     skip_group_check=True)
                    for c in range(2):
                        at_block = big[:, bass.ds(step.window + c, 1), :].rearrange("p b f -> p (b f)")
                        for j in range(G):
                            mm = nc.tensor.matmul(bank[:, j * 2 * D:(j + 1) * 2 * D], onehot_t[:, step.par, c, j * P:(j + 1) * P],
                                                  at_block, start=False, stop=(c == 1), skip_group_check=True)
                    mm.then_inc(s.s_projected, 1)

                def turn_top(step):
                    pe.wait_ge(s.s_logits, step.n + 2)
                    nc.tensor.matmul(psum[7][0:1, 0:P], peak[step.par], ident[:, :], start=True, stop=True,
                                     skip_group_check=True).then_inc(s.s_top_turned, 1)

                def spread_top(step):
                    pe.wait_ge(s.s_top, step.n)
                    pe.wait_ge(s.s_weighted, step.n + 1)
                    nc.tensor.matmul(psum[7][:, P:P + 1], ones[0:1, :], top, start=True, stop=True,
                                     skip_group_check=True).then_inc(s.s_top_spread, 1)

                def sums(step):
                    pe.wait_ge(s.s_message, step.n + 2)
                    sum_edges(pe, s, step, lambda j: message[step.par][:, j, :], D + 1)

                edge_pass(pe, [(project, 1), (sums, 3), (turn_top, 2), (turn, 0), (turn_feats, 0), (spread_top, 2)],
                          serial=[turn, turn_feats, project, turn_top, spread_top, sums])
                pe.wait_ge(s.s_sum, 1)
                nc.tensor.matmul(psum[7][:, 0:1], ones[:, :], total[:, 0:1], start=True, stop=True).then_inc(s.s_sum, 1)
                with pe.Fori(0, CHUNKS) as c:
                    def vector_event(k):
                        pe.wait_ge(s.s_upd_dve, 4 * c + 1 + k)

                    def copied(k):
                        pe.wait_ge(s.s_upd_act, UPD_ACT * c + 1 + k)

                    def event(ins):
                        ins.then_inc(s.s_upd_pe, 1)

                    vector_event(1)
                    event(turn_pairs(hc))
                    copied(2)
                    event(times_pairs("L1_gnn_W2"))
                    vector_event(2)
                    event(turn_pairs(hc))
                    copied(3)
                    event(times_pairs("Wu1_sum", stop=False))
                    event(turn_pairs(work[:, 1, :]))
                    copied(4)
                    event(times_pairs("Wu1_node", start=False))
                    vector_event(4)
                    event(turn_pairs(hc))
                    copied(6)
                    event(times_pairs("L1_gnn_Wu2"))

            return {"sync": sync, "gpsimd": gpsimd, "vector": vector, "scalar": scalar, "tensor": tensor}

        class Head(Layer):
            def __init__(self, n, at=0):
                super().__init__(n, at)
                self.s_masks = sem(n + "mask")
                self.s_spread = sem(n + "spr")
                self.s_top = sem(n + "top")
                self.s_gathered = sem(n + "gat")
                self.s_scored = sem(n + "sco")
                self.s_weighted = sem(n + "wei")

        def head():
            s = Head("head_")
            W = D + 2
            staging = rows[:, :, :, :].rearrange("p a j f -> p (a j f)")[:, 0:CB * W]
            masks = scratch[:, 0:2 * G * P]
            peaks = big[:, :, 0:2]
            seg, new, drop = ([tiny[:, k + 2 * i:k + 2 * i + 2] for i in range(2)] for k in (0, 8, 16))
            coef = [tiny[:, 24 + 2 * i:26 + 2 * i] for i in range(2)]
            z, e, t = (tiny[:, k:k + G] for k in (32, 40, 48))
            to_exp = [tiny[:, 56 + G * i:56 + G * i + G] for i in range(2)]
            weights = [tiny[:, 72 + G * i:72 + G * i + G] for i in range(2)]

            def sync(sp):
                write_table(sp, s.s_made, s.s_table, tables[5], lambda c: v3(staging, W))

            def gpsimd(pool):
                pool.wait_ge(s.s_table, 16 * (CHUNKS + 1))
                gather_pass(pool, tables[5], W, s.s_rows, s.s_message, s.s_staged)

            def vector(dve):
                before = norms_before(2)
                dve.sem_inc(s.s_table, 16)
                first = Link(dve, s.s_acc)
                first(nc.vector.memset(acc[:, :, :], 0.0))
                first(nc.vector.memset(peaks, -HUGE))
                LINKS = NORM_LINKS + 6
                with dve.Fori(0, CHUNKS) as c:
                    link = Link(dve, s.s_link, c * LINKS)
                    relu_layernorm(dve, link, c, before)
                    dve.wait_ge(s.s_table, 16 * (c + 1))
                    to, hv = v3(staging, W), v3(hc[:, :])
                    link(nc.vector.tensor_copy(to[:, :, 0:D], hv))
                    link(nc.vector.memset(to[:, :, D:D + 1], 1.0))
                    for name, out in (("L2_source", to[:, :, D + 1:D + 2]), ("L2_dest", peaks[:, bass.ds(CB * c, CB), 0:1])):
                        link(nc.vector.tensor_tensor(v3(work[:, 0, :]), hv, vector_of(name, CB), ALU.mult))
                        out = out.rearrange("p b a -> p (b a)")
                        link(nc.vector.tensor_reduce(out, v3(work[:, 0, :]), AX.X, ALU.add))
                    dve.sem_inc(s.s_made, 1)
                dve.wait_ge(s.s_table, 16 * (CHUNKS + 1))
                scores = peaks[:, 0:NB, 0:1].rearrange("p b a -> p (b a)")
                first(nc.vector.tensor_scalar(scores, scores, consts[:, 0:1], None, ALU.add))
                for credited, n in ((s.s_summed, SLOTS), (s.s_added, 2), (s.s_turned_copied, 1), (s.s_top, 1),
                                    (s.s_gathered, 2), (s.s_scored, 2), (s.s_weighted, 2), (s.s_message, SLOTS)):
                    dve.sem_inc(credited, n)

                def raise_peaks(step):
                    dve.wait_ge(s.s_masks, step.n)
                    dve.wait_ge(s.s_spread, step.n)
                    dve.wait_ge(s.s_gathered, step.n + 1)
                    dve.wait_ge(s.s_weighted, step.n + step.back)
                    take_waits(dve)
                    link = Link(dve, s.s_plink, 5 * (step.n - 1))
                    g, n, d = seg[step.par], new[step.par], drop[step.par]
                    for c in range(2):
                        part = masks[:, c * G * P:(c + 1) * G * P]
                        ins = nc.vector.tensor_tensor_reduce(part, part, psum[2][:, :], 1.0, -4 * HUGE, ALU.add, ALU.max,
                                                             g[:, c:c + 1])
                    link(ins)
                    at = peaks[:, bass.ds(step.window, 2), :]
                    own, top = (at[:, :, k:k + 1].rearrange("p b a -> p (b a)") for k in range(2))
                    link(nc.vector.tensor_tensor(g, g, own, ALU.add))
                    link(nc.vector.scalar_tensor_tensor(n, g, 0.01, g, ALU.mult, ALU.max))
                    link(nc.vector.scalar_tensor_tensor(d, n, -1.0, top, ALU.mult, ALU.add))
                    link(nc.vector.tensor_scalar(d, d, 0.0, None, ALU.min))
                    nc.vector.tensor_tensor(top, top, n, ALU.max).then_inc(s.s_top, 1)

                def score(step):
                    dve.wait_ge(s.s_rows[step.slot], 16 * G * step.fill)
                    dve.wait_ge(s.s_gathered, step.n + 2)
                    link = Link(dve, s.s_slink, 3 * (step.n - 1))
                    bank = psum[3][:, 256 * step.par:256 * step.par + 2 * G].rearrange("p (j a) -> p j a", a=2)
                    source = rows[:, step.slot, :, D + 1:D + 2].rearrange("p j a -> p (j a)")
                    own, top = (bank[:, :, k:k + 1].rearrange("p j a -> p (j a)") for k in range(2))
                    link(nc.vector.tensor_tensor(z, source, own, ALU.add))
                    link(nc.vector.scalar_tensor_tensor(e, z, 0.01, z, ALU.mult, ALU.max))
                    link(nc.vector.tensor_tensor(t, e, top, ALU.subtract))
                    nc.vector.tensor_scalar(to_exp[step.par], t, 0.0, None, ALU.min).then_inc(s.s_scored, 1)

                def weigh(step):
                    dve.wait_ge(s.s_weighted, step.n + 2)
                    dve.wait_ge(s.s_summed, step.n + 2 + step.back)
                    nc.vector.tensor_tensor(message[step.par], rows[:, step.slot, :, 0:D + 1],
                                            weights[step.par][:, :, None].to_broadcast([P, G, D + 1]),
                                            ALU.mult).then_inc(s.s_message, 1)

                def add_sums(step):
                    add_scaled(dve, s, step, coef[step.par], D + 1)

                make = onehot_stage(dve, s)
                edge_pass(dve, [(weigh, 2), (make, 0), (raise_peaks, 1), (add_sums, 2), (score, 1)],
                          serial=[make, raise_peaks, score, weigh, add_sums])
                with dve.Fori(0, CHUNKS) as c:
                    link = Link(dve, s.s_link, CHUNKS * LINKS + 4 * c)
                    total = stat[:, 0, :]
                    link(nc.vector.tensor_scalar(total, chunk(acc, c, D + 1)[:, :, D:D + 1].rearrange("p b a -> p (b a)"), 1.0e-30,
                                                 None, ALU.max))
                    link(nc.vector.reciprocal(total, total))
                    link(nc.vector.tensor_tensor(v3(hc[:, :]), chunk(acc, c), total[:, :, None].to_broadcast([P, CB, D]),
                                                 ALU.mult))
                    link(nc.vector.tensor_tensor(chunk(x, c), chunk(x, c), v3(hc[:, :]), ALU.add))

            def scalar(act):
                before = norms_before(2)
                with act.Fori(0, CHUNKS) as c:
                    root_of_var(act, c, before)

                def copy_onehot(step):
                    act.wait_ge(s.s_onehot_turned, step.n)
                    act.wait_ge(s.s_top, step.n)
                    for c in range(2):
                        ins = nc.scalar.activation(masks[:, c * G * P:(c + 1) * G * P], psum[c][:, :], ACT.Copy, bias=-HUGE,
                                                   scale=HUGE)
                    ins.then_inc(s.s_masks, 1)
                    act.wait_ge(s.s_gathered, step.n + step.back)
                    for c in range(2):
                        ins = nc.scalar.activation(onehot_t[:, step.par, c, :], psum[c][:, :], ACT.Copy)
                    ins.then_inc(s.s_turned_copied, 1)

                def exps(step):
                    act.wait_ge(s.s_scored, step.n + 2)
                    act.wait_ge(s.s_top, step.n + 1)
                    act.wait_ge(s.s_message, step.n + 2 + step.back)
                    act.wait_ge(s.s_added, step.n + step.back)
                    nc.scalar.activation(coef[step.par], drop[step.par], ACT.Exp)
                    nc.scalar.activation(weights[step.par], to_exp[step.par], ACT.Exp).then_inc(s.s_weighted, 1)

                stage = stage_rows(act, s.s_rows, s.s_staged)
                edge_pass(act, [(copy_onehot, 0), (exps, 1), (stage, -SLOTS)], serial=[stage, copy_onehot, exps])

            def tensor(pe):
                def turn(step):
                    turn_onehot(pe, s, step).then_inc(s.s_onehot_turned, 1)

                def spread(step):
                    pe.wait_ge(s.s_rows[step.slot], 16 * G * step.fill)
                    pe.wait_ge(s.s_top, step.n)
                    for j in range(G):
                        mm = nc.tensor.matmul(psum[2][:, j * P:(j + 1) * P],
                                              rows[:, step.slot, j, D + 1:D + 2].to_broadcast([P, P]), ident[:, :],
                                              start=True, stop=True)
                    mm.then_inc(s.s_spread, 1)

                def gather(step):
                    pe.wait_ge(s.s_top, step.n + 1)
                    pe.wait_ge(s.s_turned_copied, step.n + 1)
                    pe.wait_ge(s.s_scored, step.n + step.back)
                    for j in range(G):
                        for c in range(2):
                            at = 256 * step.par + 2 * j
                            mm = nc.tensor.matmul(psum[3][:, at:at + 2], onehot_t[:, step.par, c, j * P:(j + 1) * P],
                                                  peaks[:, bass.ds(step.window + c, 1), :].rearrange("p b a -> p (b a)"),
                                                  start=(c == 0), stop=(c == 1), skip_group_check=True)
                    mm.then_inc(s.s_gathered, 1)

                def sums(step):
                    pe.wait_ge(s.s_message, step.n + SLOTS)
                    sum_edges(pe, s, step, lambda j: message[step.par][:, j, :], D + 1)

                edge_pass(pe, [(sums, 2), (turn, 0), (gather, 1), (spread, 0)], serial=[turn, spread, gather, sums])

            return {"sync": sync, "gpsimd": gpsimd, "vector": vector, "scalar": scalar, "tensor": tensor}

        class Attention(Layer):
            def __init__(self, n, at=0):
                super().__init__(n, at)
                self.s_product = sem(n + "product")
                self.s_kept = sem(n + "kept")
                self.s_feats = [sem(n + f"feats{i}") for i in range(SLOTS)]
                self.s_feats_turned = sem(n + "ft")
                self.s_feats_copied = sem(n + "fc")
                self.s_gathered = sem(n + "gat")
                self.s_scored = sem(n + "sco")
                self.s_weighted = sem(n + "wei")

        def attention():
            s = Attention("att_", CHUNKS * (4 * (0 in layers) + (1 in layers)))
            staging = rows[:, :, :, :].rearrange("p a j f -> p (a j f)")[:, 0:CB * 2 * D]
            scores = [tiny[:, i * 64:i * 64 + G * HEADS] for i in range(2)]
            weights = [tiny[:, 128 + i * 64:128 + i * 64 + G * HEADS] for i in range(2)]

            def sync(sp):
                write_table(sp, s.s_made, s.s_table, tables[6], lambda c: v3(staging, 2 * D))
                load_features(sp, io["edge_attr_64"], s.s_feats, s.s_feats_turned)

            def gpsimd(pool):
                pool.wait_ge(s.s_table, 16 * (CHUNKS + 1))
                gather_pass(pool, tables[6], 2 * D, s.s_rows, s.s_message, s.s_staged)

            def vector(dve):
                before = norms_before(3)
                dve.sem_inc(s.s_table, 16)
                nc.vector.memset(acc[:, :, :], 0.0).then_inc(s.s_acc, 1)
                with dve.Fori(0, CHUNKS) as c:
                    dve.wait_ge(s_turned, c + s.at + 1)
                    link = Link(dve, s.s_link, c * NORM_LINKS)
                    relu_layernorm(dve, link, c, before)
                    dve.sem_inc(s_hc, 1)
                    dve.wait_ge(s.s_product, 2 * c + 1)
                    for bank, b, n in NARROW:
                        ins = nc.vector.tensor_tensor(big[:, bass.ds(CB * c + b, n), 0:D], v3(psum[bank][:, 0:n * D]),
                                                      vector_of("L3_gnn_bQ", n), ALU.add)
                    ins.then_inc(s.s_kept, 1)
                    dve.wait_ge(s.s_product, 2 * c + 2)
                    dve.wait_ge(s.s_table, 16 * (c + 1))
                    for bank, b, n in WIDE:
                        ins = nc.vector.tensor_tensor(v3(staging, 2 * D)[:, b:b + n, :], v3(psum[bank][:, 0:n * 2 * D], 2 * D),
                                                      vector_of("L3_gnn_bK", n, 2), ALU.add)
                    ins.then_inc(s.s_made, 1)
                dve.wait_ge(s.s_made, CHUNKS)
                dve.wait_ge(s.s_kept, CHUNKS)
                dve.wait_ge(s.s_acc, 1)
                dve.wait_ge(s.s_table, 16 * (CHUNKS + 1))
                for credited, n in ((s.s_summed, SLOTS), (s.s_added, 2), (s.s_turned_copied, 1), (s.s_feats_turned, SLOTS),
                                    (s.s_feats_copied, 1), (s.s_gathered, 2), (s.s_scored, 2), (s.s_message, SLOTS)):
                    dve.sem_inc(credited, n)

                def score(step):
                    dve.wait_ge(s.s_rows[step.slot], 16 * G * step.fill)
                    dve.wait_ge(s.s_gathered, step.n + 2)
                    dve.wait_ge(s.s_weighted, step.n)
                    link = Link(dve, s.s_slink, 4 * (step.n - 1))
                    p, bank, sc = product, psum[2 + step.par], scores[step.par]
                    link(nc.vector.tensor_tensor(v3(p), rows[:, step.slot, :, 0:D], v3(bank[:, 0:G * D]), ALU.mult))
                    link(nc.vector.tensor_tensor(p, p, bank[:, G * D:2 * G * D], ALU.mult))
                    link(nc.vector.tensor_reduce(sc, p.rearrange("p (h d) -> p h d", d=D // HEADS), AX.X, ALU.add))
                    link(nc.vector.tensor_scalar(sc, sc, float((D // HEADS) ** -0.5), -5.0, ALU.mult, ALU.max))
                    nc.vector.tensor_scalar(sc, sc, 5.0, None, ALU.min).then_inc(s.s_scored, 1)

                def weigh(step):
                    dve.wait_ge(s.s_weighted, step.n + 2)
                    dve.wait_ge(s.s_summed, step.n + 2 + step.back)
                    value = rows[:, step.slot, :, D:2 * D].rearrange("p j (h d) -> p j h d", h=HEADS)
                    w = weights[step.par].rearrange("p (j h) -> p j h", h=HEADS)[:, :, :, None].to_broadcast([P, G, HEADS, D // HEADS])
                    to = message[step.par][:, :, 0:D].rearrange("p j (h d) -> p j h d", h=HEADS)
                    nc.vector.tensor_tensor(to, value, w, ALU.mult).then_inc(s.s_message, 1)

                def add_sums(step):
                    dve.wait_ge(s.s_summed, step.n + SLOTS)
                    dve.wait_ge(s.s_added, step.n + 1)
                    to = acc[:, bass.ds(step.window, 2), 0:D]
                    nc.vector.tensor_tensor(to, to, v3(psum[4 + step.par][:, 0:2 * D]), ALU.add).then_inc(s.s_added, 1)

                make = onehot_stage(dve, s)
                edge_pass(dve, [(weigh, 2), (make, 0), (score, 1), (add_sums, 2)], serial=[make, score, weigh, add_sums])
                with dve.Fori(0, CHUNKS) as c:
                    link = Link(dve, s.s_link, CHUNKS * NORM_LINKS + c)
                    link(nc.vector.tensor_tensor(chunk(x, c), chunk(x, c), chunk(acc, c), ALU.add))

            def scalar(act):
                before = norms_before(3)
                with act.Fori(0, CHUNKS) as c:
                    root_of_var(act, c, before)
                    act.wait_ge(s_turned, c + s.at + 2)
                    copy_turned().then_inc(s_ht, 1)
                act.sem_inc(s.s_weighted, 2)

                def copy_onehot(step):
                    act.wait_ge(s.s_onehot_turned, step.n)
                    act.wait_ge(s.s_gathered, step.n + step.back)
                    for c in range(2):
                        ins = nc.scalar.activation(onehot_t[:, step.par, c, :], psum[c][:, :], ACT.Copy)
                    ins.then_inc(s.s_turned_copied, 1)

                def copy_feats(step):
                    act.wait_ge(s.s_feats_turned, step.n + SLOTS)
                    nc.scalar.activation(feats_t[step.par], psum[6][:, 0:2 * P], ACT.Copy).then_inc(s.s_feats_copied, 1)

                def exps(step):
                    act.wait_ge(s.s_scored, step.n + 2)
                    act.wait_ge(s.s_message, step.n + 2 + step.back)
                    nc.scalar.activation(weights[step.par], scores[step.par], ACT.Exp).then_inc(s.s_weighted, 1)

                stage = stage_rows(act, s.s_rows, s.s_staged)
                edge_pass(act, [(copy_onehot, 0), (copy_feats, 0), (exps, 1), (stage, -SLOTS)],
                          serial=[stage, copy_onehot, copy_feats, exps])

            def tensor(pe):
                with pe.Fori(0, CHUNKS) as c:
                    pe.wait_ge(s_hc, c + s.at + 1)
                    turn_pairs(hc).then_inc(s_turned, 1)
                    pe.wait_ge(s_ht, c + s.at + 1)
                    times_pairs("L3_gnn_WQ").then_inc(s.s_product, 1)
                    pe.wait_ge(s.s_kept, c + 1)
                    times_wide("key_value").then_inc(s.s_product, 1)

                def turn(step):
                    turn_onehot(pe, s, step).then_inc(s.s_onehot_turned, 1)

                def turn_feats(step):
                    pe.wait_ge(s.s_feats[step.slot], 16 * step.fill)
                    pe.wait_ge(s.s_feats_copied, step.n)
                    for half in range(2):
                        mm = nc.tensor.transpose(psum[6][:, half * P:(half + 1) * P],
                                                 feats[:, step.slot, 2 * half:2 * half + 2, :].rearrange("p j f -> p (j f)"),
                                                 ident[:, :])
                    mm.then_inc(s.s_feats_turned, 1)

                def gather_and_project(step):
                    pe.wait_ge(s.s_turned_copied, step.n + 1)
                    pe.wait_ge(s.s_feats_copied, step.n + 1)
                    pe.wait_ge(s.s_scored, step.n + step.back)
                    bank = psum[2 + step.par]
                    for half in range(2):
                        nc.tensor.matmul(bank[:, (2 + half) * P:(3 + half) * P], feats_t[step.par][:, half * P:(half + 1) * P],
                                         pair_w[:, PAIR_W["L3_gnn_WE"], :, :], start=(half == 0), stop=False,
                                         skip_group_check=True)
                    nc.tensor.matmul(bank[:, G * D:2 * G * D], ones[0:1, :],
                                     vectors[0:1, VECTORS["L3_gnn_bE"], None, :].to_broadcast([1, G, D]),
                                     start=False, stop=True, skip_group_check=True)
                    for c in range(2):
                        at_block = big[:, bass.ds(step.window + c, 1), 0:D].rearrange("p b f -> p (b f)")
                        for j in range(G):
                            mm = nc.tensor.matmul(bank[:, j * D:(j + 1) * D], onehot_t[:, step.par, c, j * P:(j + 1) * P],
                                                  at_block, start=False, stop=(c == 1), skip_group_check=True)
                    mm.then_inc(s.s_gathered, 1)

                def sums(step):
                    pe.wait_ge(s.s_message, step.n + SLOTS)
                    sum_edges(pe, s, step, lambda j: message[step.par][:, j, 0:D], D)

                edge_pass(pe, [(sums, 2), (gather_and_project, 1), (turn, 0), (turn_feats, 0)],
                          serial=[turn, turn_feats, gather_and_project, sums])

            return {"sync": sync, "gpsimd": gpsimd, "vector": vector, "scalar": scalar, "tensor": tensor}

        s_x_done = sem("s_x_done")
        convs = [Pass(f"conv{k}_", CHUNKS * k) for k in range(4)] if 0 in layers else []

        def norms_before(layer):
            return CHUNKS * sum(l < layer for l in layers)

        layer_runs = [run() for l, run in ((1, messages), (2, head), (3, attention)) if l in layers]

        block = ctx.enter_context(nc.Block())

        @block.sync
        def _(sp):
            prep_sync(sp)
            weight_loads(sp)
            for k, s in enumerate(convs):
                write_table(sp, s_conv_made, s_conv_table, tables[k], lambda c: chunk(acc, c), s.at)
            for run in layer_runs:
                run["sync"](sp)
            sp.wait_ge(s_x_done, 1)
            sp.dma_start(io["out"][0:(NB - 1) * P, :].rearrange("(b p) c -> p b c", p=P), x[:, 0:NB - 1, :]).then_inc(s_out, 16)
            sp.dma_start(io["out"][(NB - 1) * P:NODES, :], x[0:LAST, NB - 1, :]).then_inc(s_out, 16)
            sp.wait_ge(s_out, 32)

        @block.gpsimd
        def _(pool):
            prep_pool(pool)
            pool.wait_ge(s_index, 1)
            for k, s in enumerate(convs):
                pool.wait_ge(s_conv_table, 16 * (s.at + CHUNKS))
                gather_pass(pool, tables[k], D, s.s_rows, s.s_summed, s.s_staged)
            for run in layer_runs:
                run["gpsimd"](pool)

        @block.vector
        def _(dve):
            nc.vector.memset(pair_w[:, :, :, :], 0.0).then_inc(s_w0, 1)
            nc.vector.memset(wide_w[:, :, :, :], 0.0).then_inc(s_w0, 1)
            nc.vector.memset(edge_w[:, :, :], 0.0).then_inc(s_w0, 1)
            nc.vector.memset(ones[:, :], 1.0)
            nc.vector.memset(big[:, NB, :], 0.0).then_inc(s_w0, 1)
            prep_vector(dve)
            dve.wait_ge(s_w, 16 * WEIGHT_LOADS)
            dve.wait_ge(s_x, 32)
            for k, s in enumerate(convs):
                conv_vector(dve, k, s)
            if convs:
                conv_end_vector(dve)
            for run in layer_runs:
                run["vector"](dve)
            dve.sem_inc(s_x_done, 1)

        @block.scalar
        def _(act):
            act.wait_ge(s_index, 1)
            for k, s in enumerate(convs):
                conv_scalar(act, k, s)
            if not convs:
                act.wait_ge(s_degrees, 1)
                nc.scalar.activation(dis[:, :], dis[:, :], ACT.Sqrt).then_inc(s_dis, 1)
            for run in layer_runs:
                run["scalar"](act)

        @block.tensor
        def _(pe):
            prep_tensor(pe)
            pe.wait_ge(s_index, 1)
            pe.wait_ge(s_w, 16 * WEIGHT_LOADS)
            pe.sem_inc(s_turned, 1)
            for k, s in enumerate(convs):
                conv_tensor(pe, k, s)
            for run in layer_runs:
                run["tensor"](pe)


_INS = ["x", "src", "dst", "edge_attr_32", "edge_attr_64",
        "L0_gnn_W1", "L0_gnn_b1", "L0_gnn_W2", "L0_gnn_b2", "L0_gnn_W3", "L0_gnn_b3", "L0_gnn_W4", "L0_gnn_b4",
        "L1_gnn_W1", "L1_gnn_b1", "L1_gnn_W2", "L1_gnn_b2", "L1_gnn_Wa1", "L1_gnn_ba1", "L1_gnn_Wa2", "L1_gnn_ba2",
        "L1_gnn_Wu1", "L1_gnn_bu1", "L1_gnn_Wu2", "L1_gnn_bu2", "L2_gnn_W", "L2_gnn_b",
        "L3_gnn_WQ", "L3_gnn_bQ", "L3_gnn_WK", "L3_gnn_bK", "L3_gnn_WE", "L3_gnn_bE", "L3_gnn_WV", "L3_gnn_bV"]
_OUTS = [((NODES, D), "float32")]


def kernel(**inputs):
    import numpy as _np
    import concourse.bacc as _bacc
    from concourse import mybir as _mybir
    from concourse.bass_utils import run_bass_kernel_spmd as _run

    nc = _bacc.Bacc("TRN2", target_bir_lowering=False, num_devices=1)
    arrays, io = {}, {}
    for name in _INS:
        a = _np.ascontiguousarray(inputs[name])
        arrays[f"in_{name}"] = a
        io[name] = nc.dram_tensor(f"in_{name}", a.shape, _mybir.dt.from_np(a.dtype), kind="ExternalInput").ap()
    shape, dtype = _OUTS[0]
    io["out"] = nc.dram_tensor("out_0", shape, _mybir.dt.from_np(_np.dtype(dtype)), kind="ExternalOutput").ap()
    gnn_program(nc, io["src"], io["dst"], io)
    r = _run(nc, [arrays], core_ids=[0])
    return r.results[0]["out_0"]
```

```python
import concourse.bass as bass
from concourse import mybir
from contextlib import ExitStack
from collections import namedtuple

F32 = mybir.dt.float32
BF16 = mybir.dt.bfloat16
I32 = mybir.dt.int32
ALU = mybir.AluOpType
ACT = mybir.ActivationFunctionType
AX = mybir.AxisListType

NODES = 12500
EDGES = 200000
P = 128
D = 64
ED1 = 32
HEADS = 8

G = 4
GE = G * P
SLOTS = 4
UNROLL = 8
NG = -(-EDGES // (GE * UNROLL)) * UNROLL
FULL = EDGES // GE
TAIL = EDGES - FULL * GE
REPEATED = (GE - TAIL) // G
QG = NG // SLOTS
NB = -(-NODES // P)
NBW = NB + 1
LAST = NODES - (NB - 1) * P
CB = 14
CHUNKS = NB // CB
IDLE_PRODUCTS = {1: 3, 2: 8, 3: 5}
PAIRS = CB // 2
WIN = 2 * P
NOWHERE = -4096.0
HUGE = 1.0e30
EPS = 1.0e-5
assert NG - FULL == 2 and UNROLL % SLOTS == 0 and TAIL % G == 0 and NB % CB == 0 and EDGES % GE == TAIL

PAIR_W = {"L0_gnn_W1": 0, "L0_gnn_W2": 1, "L0_gnn_W3": 2, "L0_gnn_W4": 3, "L1_gnn_W2": 4, "Wu1_node": 5, "Wu1_sum": 6,
          "L1_gnn_Wu2": 7, "L3_gnn_WQ": 8, "L3_gnn_WE": 9}
WIDE_W = {"sender": 0, "receiver": 1, "key_value": 2}
VECTORS = {"L0_gnn_b1": 0, "L0_gnn_b2": 1, "L0_gnn_b3": 2, "L0_gnn_b4": 3, "L1_gnn_b1": 4, "L1_gnn_ba1": 5, "L1_gnn_b2": 6,
           "L1_gnn_bu1": 7, "L1_gnn_bu2": 8, "L1_gnn_Wa2": 9, "L2_source": 10, "L2_dest": 11, "L3_gnn_bK": 12,
           "L3_gnn_bV": 13, "L3_gnn_bQ": 14, "L3_gnn_bE": 15}

Step = namedtuple("Step", "n group window last slot par fill back")


def gnn_program(nc, src, dst, io, layers=(0, 1, 2, 3)):
    ctx = ExitStack()
    with ctx:
        def sb(name, shape, dt=F32):
            return ctx.enter_context(nc.sbuf_tensor("sb_" + name, shape, dt))

        def sem(name):
            return ctx.enter_context(nc.semaphore(name))

        x = sb("x", [P, NB, D])
        h = sb("h", [P, NB, D])
        acc = sb("acc", [P, NBW, D + 1])
        big = sb("big", [P, NBW, 2 * D])
        dis = sb("dis", [P, NB])
        dst_at = sb("dst_at", [P, NG, G])
        row_at = sb("row_at", [P, NG, G], I32)
        win_row = sb("win_row", [1, NG + UNROLL, 2], I32)
        more = sb("more", [1, 8], I32)
        row_now = sb("row_now", [P, SLOTS, G], I32)
        rows = sb("rows", [P, SLOTS, G, 2 * D])
        feats = sb("feats", [P, SLOTS, G, D])
        onehot = sb("onehot", [P, SLOTS, G, WIN])
        onehot_t = sb("onehot_t", [P, 2, 2, G * P])
        work = sb("work", [P, 2, CB * D])
        hc = sb("hc", [P, CB * D])
        ht = sb("ht", [P, CB * D])
        iota = sb("iota", [P, WIN])
        iota16 = sb("iota16", [P, P], BF16)
        minus_block = sb("minus_block", [P, NBW])
        from_middle = sb("from_middle", [P, NBW])
        minus_half = sb("minus_half", [P, 1])
        ident = sb("ident", [P, P])
        bias16 = sb("bias16", [P, D], BF16)
        zeros16 = sb("zeros16", [P, P], BF16)
        ones = sb("ones", [P, P])
        pair_w = sb("pair_w", [P, len(PAIR_W), 2, D])
        wide_w = sb("wide_w", [P, len(WIDE_W), 2, 2 * D])
        edge_w = sb("edge_w", [P, G, 2 * D])
        stat = sb("stat", [P, 3, CB])
        vectors = sb("vectors", [P, len(VECTORS), D])
        consts = sb("consts", [P, 2])
        ident16, ones16 = (t[:, :].bitcast(BF16)[:, 1:2 * P:2] for t in (ident, ones))
        psum = [ctx.enter_context(nc.psum_tensor(f"bank{i}", [P, 512], F32)) for i in range(8)]

        tables = [nc.dram_tensor(f"table{i}", [P, NB, w], F32, kind="Internal").ap()
                  for i, w in enumerate([D, D, D, D, 2 * D, D + 4, 2 * D])]

        raw = big[:, :, :].rearrange("p b f -> p (b f)")
        raw_dst = raw[0:QG, 0:SLOTS * GE].bitcast(I32).rearrange("p (q e) -> p q e", e=GE)
        raw_src = raw[0:QG, SLOTS * GE:2 * SLOTS * GE].bitcast(I32).rearrange("p (q e) -> p q e", e=GE)
        part = raw[0:QG, 2 * SLOTS * GE:3 * SLOTS * GE].bitcast(I32).rearrange("p (q e) -> p q e", e=GE)
        flat = h[:, :, :].rearrange("p b f -> p (b f)")
        hi_f = flat[0:QG, 0:2048].rearrange("p (q e) -> p q e", e=GE)
        lo_f = flat[0:QG, 2048:4096].rearrange("p (q e) -> p q e", e=GE)
        row_f = flat[0:QG, 4096:6144].rearrange("p (q e) -> p q e", e=GE)
        assert SLOTS * GE == 2048
        acc_flat = acc[:, :, :].rearrange("p b f -> p (b f)")
        hi_at = acc_flat[:, 0:NG * G].rearrange("p (g j) -> p g j", j=G)
        lo_at = acc_flat[:, NG * G:2 * NG * G].rearrange("p (g j) -> p g j", j=G)
        lo16 = acc_flat[:, 2 * NG * G:2 * NG * G + NG * G // 2].bitcast(BF16).rearrange("p (g j) -> p g j", j=G)
        minus_index = acc_flat[:, 3 * NG * G:3 * NG * G + NBW]
        oh16 = onehot[:, :, :, :].rearrange("p a g w -> p a (g w)").bitcast(BF16)
        lim = stat[0:QG, 0:2, 0:SLOTS]

        s_raw = sem("s_raw")
        s_x = sem("s_x")
        s_x0 = sem("s_x0")
        s_const = sem("s_const")
        s_constf = sem("s_constf")
        s_prep = sem("s_prep")
        s_split = sem("s_split")
        s_quarter = sem("s_quarter")
        s_kept = sem("s_kept")
        s_lim = sem("s_lim")
        s_limrow = sem("s_limrow")
        s_index = sem("s_index")
        s_oh16 = sem("s_oh16")
        s_counted = sem("s_counted")
        s_deg = sem("s_deg")
        s_degrees = sem("s_degrees")
        s_dis = sem("s_dis")
        s_out = sem("s_out")

        def quarter_loads(eng, of, to):
            for q in range(SLOTS - 1):
                at = q * QG * GE
                eng.dma_start(to[:, q, :], of[at:at + QG * GE].rearrange("(g e) -> g e", e=GE)).then_inc(s_raw, 16)
            at = (SLOTS - 1) * QG * GE
            left = FULL - (SLOTS - 1) * QG
            eng.dma_start(to[0:left, SLOTS - 1, :], of[at:at + left * GE].rearrange("(g e) -> g e", e=GE)).then_inc(s_raw, 16)
            for g in range(left, QG):
                eng.dma_start(to[g:g + 1, SLOTS - 1, :], of[EDGES - GE:EDGES].rearrange("(g e) -> g e", e=GE)).then_inc(s_raw, 16)

        RAW_LOADS = 2 * (SLOTS + QG - (FULL - (SLOTS - 1) * QG))

        def prep_sync(sp):
            quarter_loads(sp, dst, raw_dst)
            quarter_loads(sp, src, raw_src)
            sp.dma_start(x[:, 0:NB - 1, :], io["x"][0:(NB - 1) * P, :].rearrange("(b p) c -> p b c", p=P)).then_inc(s_x, 16)
            sp.wait_ge(s_x0, 1)
            sp.dma_start(x[0:LAST, NB - 1, :], io["x"][(NB - 1) * P:NODES, :]).then_inc(s_x, 16)

        def prep_pool(pool):
            nc.gpsimd.memset(ident[:, :], 0.0).then_inc(s_const, 1)
            nc.gpsimd.memset(zeros16[:, :], 0.0).then_inc(s_const, 1)
            nc.gpsimd.iota(iota[:, :], pattern=[[1, WIN]], base=0, channel_multiplier=0,
                           allow_small_or_imprecise_dtypes=True).then_inc(s_const, 1)
            nc.gpsimd.iota(minus_block[:, :], pattern=[[-P, NBW]], base=0, channel_multiplier=0,
                           allow_small_or_imprecise_dtypes=True).then_inc(s_const, 1)
            pool.wait_ge(s_const, 4)
            nc.gpsimd.tensor_copy(iota16[:, :], iota[:, 0:P]).then_inc(s_const, 1)
            nc.gpsimd.affine_select(out=ident[:, :], in_=ident[:, :], compare_op=ALU.not_equal, fill=1.0, base=0,
                                    pattern=[[-1, P]], channel_multiplier=1).then_inc(s_const, 1)

        CONSTS = 6

        class Link:
            def __init__(self, eng, s, base=0):
                self.eng, self.s, self.base, self.k = eng, s, base, 0

            def __call__(self, ins):
                ins.then_inc(self.s, 1)
                self.k += 1
                self.eng.wait_ge(self.s, self.base + self.k)

        def prep_vector(dve):
            nc.vector.memset(x[:, NB - 1, :], 0.0).then_inc(s_x0, 1)
            link = Link(dve, s_prep)
            dve.wait_ge(s_raw, 16 * RAW_LOADS)
            link(nc.vector.tensor_scalar(part, raw_dst, 7, None, ALU.arith_shift_right))
            link(nc.vector.tensor_copy(hi_f, part))
            link(nc.vector.tensor_scalar(part, raw_dst, P - 1, None, ALU.bitwise_and))
            nc.vector.tensor_copy(lo_f, part).then_inc(s_split, 1)
            nc.vector.tensor_reduce(lim[:, 0, :], hi_f, AX.X, ALU.min)
            nc.vector.tensor_reduce(lim[:, 1, :], hi_f, AX.X, ALU.max).then_inc(s_lim, 1)
            dve.wait_ge(s_split, 1)
            link(nc.vector.tensor_scalar(part, raw_src, P - 1, None, ALU.bitwise_and))
            link(nc.vector.tensor_scalar(row_f, part, float(NB), None, ALU.mult))
            link(nc.vector.tensor_scalar(part, raw_src, 7, None, ALU.arith_shift_right))
            nc.vector.tensor_tensor(row_f, row_f, part, ALU.add).then_inc(s_split, 1)
            k = 0
            for to in (hi_at, lo_at, row_at):
                for q in range(SLOTS):
                    k += 1
                    dve.wait_ge(s_quarter, k)
                    bank = psum[k % 2][:, 0:G * QG].rearrange("p (j g) -> p g j", g=QG)
                    nc.vector.tensor_copy(to[:, q * QG:(q + 1) * QG, :], bank).then_inc(s_kept, 1)
            dve.wait_ge(s_kept, k)
            link(nc.vector.scalar_tensor_tensor(dst_at[:, :, :], hi_at, float(P), lo_at, ALU.mult, ALU.add))
            link(nc.vector.memset(dst_at[0:REPEATED, FULL, :], NOWHERE))
            link(nc.vector.memset(dst_at[:, FULL + 1, :], NOWHERE))
            for at in (hi_at, lo_at):
                link(nc.vector.memset(at[0:REPEATED, FULL, :], -1.0))
                link(nc.vector.memset(at[:, FULL + 1, :], -1.0))
            link(nc.vector.tensor_copy(lo16, lo_at))
            link(nc.vector.tensor_scalar(minus_index, minus_block[:, :], 1.0 / P, None, ALU.mult))
            dve.wait_ge(s_limrow, 1)
            link(nc.vector.memset(win_row[:, :, :], 0))
            link(nc.vector.tensor_copy(win_row[:, 0:NG, 0], psum[2][0:1, 0:NG]))
            link(nc.vector.tensor_copy(win_row[:, 0:NG, 1], psum[3][0:1, 0:NG]))
            reach = hc[0:1, 0:NG]
            link(nc.vector.tensor_copy(reach, psum[2][0:1, 0:NG]))
            link(nc.vector.tensor_tensor(reach, psum[3][0:1, 0:NG], reach, ALU.subtract))
            link(nc.vector.tensor_reduce(hc[0:1, NG:NG + 1], reach, AX.X, ALU.max))
            link(nc.vector.tensor_scalar(more[0:1, 0:1], hc[0:1, NG:NG + 1], -1.0, None, ALU.add))
            link(nc.vector.tensor_scalar(from_middle[:, :], minus_block[:, :], -(WIN - 1) / 2, None, ALU.add))
            link(nc.vector.memset(minus_half[:, :], -(WIN - 1) / 2))
            dve.sem_inc(s_index, 1)
            def build(step):
                dve.wait_ge(s_counted, step.n + step.back)
                take_waits(dve)
                buf = oh16[:, step.par]
                nc.vector.tensor_tensor(
                    buf[:, 0:G * P].rearrange("p (j w) -> p j w", w=P),
                    lo16[:, bass.ds(step.group, 1), :].rearrange("p g j -> p (g j)")[:, :, None].to_broadcast([P, G, P]),
                    iota16[:, None, :].to_broadcast([P, G, P]), ALU.is_equal)
                nc.vector.scalar_tensor_tensor(
                    buf[:, G * P:G * (P + 2)].rearrange("p (j w) -> p j w", w=2),
                    hi_at[:, bass.ds(step.group, 1), :].rearrange("p g j -> p (g j)")[:, :, None].to_broadcast([P, G, 2]),
                    minus_index[:, bass.ds(step.window, 1)], iota[:, None, 0:2].to_broadcast([P, G, 2]), ALU.add,
                    ALU.is_equal).then_inc(s_oh16, 1)

            edge_pass(dve, [(build, 0)])
            dve.wait_ge(s_deg, 1)
            link(nc.vector.tensor_scalar(dis[:, :], psum[4][:, 0:NB], 1.0, 1.0, ALU.add, ALU.max))
            dve.sem_inc(s_degrees, 1)
            dve.wait_ge(s_dis, 1)
            link(nc.vector.reciprocal(dis[:, :], dis[:, :]))
            link(nc.vector.memset(acc[:, :, :], 0.0))

        def prep_tensor(pe):
            pe.wait_ge(s_const, CONSTS)
            k = 0
            for of in (hi_f, lo_f, row_f):
                pe.wait_ge(s_split, 2 if of is row_f else 1)
                for q in range(SLOTS):
                    k += 1
                    if k > 2:
                        pe.wait_ge(s_kept, k - 2)
                    for j in range(G):
                        mm = nc.tensor.transpose(psum[k % 2][:, j * QG:(j + 1) * QG], of[:, q, j:GE:G], ident[0:QG, 0:QG])
                    mm.then_inc(s_quarter, 1)
            pe.wait_ge(s_lim, 1)
            for t in range(2):
                for q in range(SLOTS):
                    mm = nc.tensor.matmul(psum[2 + t][0:1, q * QG:(q + 1) * QG], lim[:, t, q:q + 1], ident[0:QG, 0:QG],
                                          start=True, stop=True)
            mm.then_inc(s_limrow, 1)
            pe.sem_inc(s_counted, 2)
            nc.tensor.matmul(psum[4][:, 0:NBW], zeros16[:, :], zeros16[:, 0:NBW], start=True, stop=False, skip_group_check=True)
            pe.wait_ge(s_index, 1)

            def count(step):
                pe.wait_ge(s_oh16, step.n)
                for j in range(G):
                    mm = nc.tensor.matmul(psum[4][:, bass.ds(step.window, 2)], oh16[:, step.par, j * P:(j + 1) * P],
                                          oh16[:, step.par, G * P + 2 * j:G * P + 2 * j + 2], start=False, stop=False,
                                          skip_group_check=True)
                mm.then_inc(s_counted, 1)

            edge_pass(pe, [(count, 0)])
            nc.tensor.matmul(psum[4][:, 0:NBW], zeros16[:, :], zeros16[:, 0:NBW], start=False, stop=True,
                             skip_group_check=True).then_inc(s_deg, 1)

        s_spare = sem("s_spare")

        def take_waits(eng):
            eng.sem_inc(s_spare, 1)

        named = [0]

        def register(eng, name):
            named[0] += 1
            return eng.alloc_register(f"{name}{named[0]}")

        def edge_pass(eng, stages, serial=None, skips=False):
            deepest = max(0, *(lag for _, lag in stages))
            ahead = -min(0, min(lag for _, lag in stages))
            assert ahead in (0, SLOTS) and deepest <= SLOTS
            steady = NG // UNROLL - (1 if ahead else 0)
            each = 2 if skips else 1
            regs = [register(eng, "window") for i in range(each * (UNROLL + deepest))]

            def moment(t, u, i, windows):
                for stage, lag in stages:
                    if t is not None and not 0 <= t - lag < NG:
                        continue
                    w = windows[each * (u - lag + deepest)] if lag >= 0 else None
                    last = windows[2 * (u - lag + deepest) + 1] if lag >= 0 and skips else None
                    stage(Step(n=UNROLL * i + u - lag + 1, group=UNROLL * i + u - lag, window=w, last=last,
                               slot=(u - lag) % SLOTS, par=(u - lag) % 2,
                               fill=UNROLL // SLOTS * i + 1 + (u - lag) // SLOTS, back=0))

            def load_windows(i):
                if all(lag < 0 for _, lag in stages):
                    return None
                have = regs[each * deepest:] if isinstance(i, int) and i == 0 else regs
                if isinstance(i, int) and i == 0:
                    at = win_row[0:1, 0:UNROLL, 0:each]
                else:
                    at = win_row[0:1, bass.ds(UNROLL * i - deepest, UNROLL + deepest), 0:each]
                eng.load(have, at.rearrange("a g k -> a (g k)"))
                return [None] * (len(regs) - len(have)) + [eng.snap(r, min_val=0, max_val=NB - 1) for r in have]

            for t in range(-ahead, 0):
                for stage, lag in stages:
                    if t - lag >= 0:
                        stage(Step(n=t - lag + 1, group=t - lag, window=None, last=None, slot=(t - lag) % SLOTS, par=(t - lag) % 2,
                                   fill=1 + (t - lag) // SLOTS, back=0))
            windows = load_windows(0)
            for u in range(UNROLL):
                moment(u, u, 0, windows)
            with eng.Fori(1, steady) as i:
                windows = load_windows(i)
                for u in range(UNROLL):
                    moment(None, u, i, windows)
            for t in range(UNROLL * steady, NG + deepest):
                if t % UNROLL == 0:
                    windows = load_windows(t // UNROLL)
                moment(t, t % UNROLL, t // UNROLL, windows)

            beyond(eng, lambda step: [stage(step) for stage in (serial or [stage for stage, _ in stages])])
            for r in regs:
                eng.free_register(r)

        def beyond(eng, work_on):
            count = register(eng, "count")
            eng.reg_mov(count, 0)
            ends = [register(eng, "first"), register(eng, "last")]
            some = eng.value_load(more[0:1, 0:1], min_val=-1, max_val=NB)
            with eng.If(some > 0):
                with eng.Fori(0, NG) as g:
                    eng.load([ends[0]], win_row[0:1, bass.ds(g, 1), 0])
                    eng.load([ends[1]], win_row[0:1, bass.ds(g, 1), 1])
                    first, last = (eng.snap(r, min_val=0, max_val=NB - 1) for r in ends)
                    with eng.If(first + 1 < last):
                        with eng.Fori(first + 2, last + 1, 2) as w:
                            eng.reg_add(count, count, 1)
                            k = eng.snap(count, min_val=1, max_val=NG * NB)
                            work_on(Step(n=NG + k, group=g, window=w, last=None, slot=0, par=0, fill=NG // SLOTS + k, back=1))
                    eng.reg_mov(ends[0], 0)
                eng.reg_mov(ends[0], 0)
            eng.free_register(count)
            for r in ends:
                eng.free_register(r)

        def dst_of(g):
            return dst_at[:, bass.ds(g, 1), :].rearrange("p g j -> p (g j)")

        def on_second(eng, step, work):
            if step.last is None:
                work()
            else:
                with eng.If(step.last > step.window):
                    work()

        def on_blocks(eng, step, work):
            if step.last is None:
                work(2)
            else:
                take_waits(eng)
                with eng.If(step.last > step.window):
                    work(2)
                with eng.Else():
                    work(1)

        def build_onehot(step, blocks=2):
            n = blocks * P
            return nc.vector.scalar_tensor_tensor(
                onehot[:, step.slot, :, 0:n], dst_of(step.group)[:, :, None].to_broadcast([P, G, n]),
                minus_block[:, bass.ds(step.window, 1)], iota[:, None, 0:n].to_broadcast([P, G, n]), ALU.add, ALU.is_equal)

        def gather_pass(pool, table, width, s_rows, s_free, s_staged):
            view = table.rearrange("p b f -> (p b) f")

            def fetch(slot, n, back=0):
                n, used = pool.snap(n), pool.snap(n + back)
                pool.wait_ge(s_free, used)
                pool.wait_ge(s_staged, n)
                take_waits(pool)
                for j in range(G):
                    nc.gpsimd.indirect_dma_start(
                        out=rows[:, slot, j, 0:width], out_offset=None, in_=view,
                        in_offset=bass.IndirectOffsetOnAxis(ap=row_now[:, slot, j:j + 1], axis=0),
                        bounds_check=P * NB - 1).then_inc(s_rows[slot], 16)

            with pool.Fori(0, NG // SLOTS) as i:
                for u in range(SLOTS):
                    fetch(u, SLOTS * i + u + 1)
            beyond(pool, lambda step: fetch(0, step.n, SLOTS - 1))

        def stage_rows(act, s_rows, s_staged):
            def stage(step):
                if not (isinstance(step.fill, int) and step.fill == 1):
                    act.wait_ge(s_rows[step.slot], 16 * G * (step.fill - 1))
                take_waits(act)
                at = row_at[:, bass.ds(step.group, 1), :].rearrange("p g j -> p (g j)")
                nc.scalar.activation(row_now[:, step.slot, :], at, ACT.Copy).then_inc(s_staged, 1)

            return stage

        s_w0, s_w = sem("s_w0"), sem("s_w")
        s_var = sem("s_var")
        s_rstd = sem("s_rstd")
        NORM_LINKS = 7

        def weight_loads(sp):
            sp.wait_ge(s_w0, 3)
            n = 0

            def load(to, of):
                nonlocal n
                sp.dma_start(to, of).then_inc(s_w, 16)
                n += 1

            u1 = io["L1_gnn_Wu1"]
            for name, at in PAIR_W.items():
                w = {"Wu1_node": u1[0:D, :], "Wu1_sum": u1[D:2 * D, :]}.get(name, io[name] if name in io else None)
                for half in range(2):
                    load(pair_w[D * half:D * half + D, at, half, :], w)
            for half in range(2):
                rows_of = slice(D * half, D * half + D)
                for part, name in enumerate(("L1_gnn_W1", "L1_gnn_Wa1")):
                    cols = slice(D * part, D * part + D)
                    load(wide_w[rows_of, WIDE_W["sender"], half, cols], io[name][0:D, :])
                    load(wide_w[rows_of, WIDE_W["receiver"], half, cols], io[name][D:2 * D, :])
                for part, name in enumerate(("L3_gnn_WK", "L3_gnn_WV")):
                    load(wide_w[rows_of, WIDE_W["key_value"], half, D * part:D * part + D], io[name])
            for j in range(G):
                for part, name in enumerate(("L1_gnn_W1", "L1_gnn_Wa1")):
                    load(edge_w[ED1 * j:ED1 * j + ED1, j, D * part:D * part + D], io[name][2 * D:2 * D + ED1, :])
            for name, at in VECTORS.items():
                if name == "L2_source":
                    v = io["L2_gnn_W"][0:1, 0:D]
                elif name == "L2_dest":
                    v = io["L2_gnn_W"][0:1, D:2 * D]
                elif name == "L1_gnn_Wa2":
                    v = io[name].rearrange("f a -> a f")
                else:
                    v = io[name].rearrange("(a f) -> a f", a=1)
                load(vectors[:, at, :], v.to_broadcast([P, D]))
            load(consts[:, 0:1], io["L2_gnn_b"].rearrange("(a f) -> a f", a=1).to_broadcast([P, 1]))
            load(consts[:, 1:2], io["L1_gnn_ba2"].rearrange("(a f) -> a f", a=1).to_broadcast([P, 1]))
            assert n == WEIGHT_LOADS

        WEIGHT_LOADS = 2 * len(PAIR_W) + 12 + 2 * G + len(VECTORS) + 2

        def chunk(t, c, width=D):
            return t[:, bass.ds(CB * c, CB), 0:width]

        def v3(t, f=D):
            return t.rearrange("p (b f) -> p b f", f=f)

        def vector_of(name, n, width=1):
            at = VECTORS[name]
            return vectors[:, at:at + width, :].rearrange("p a f -> p (a f)")[:, None, :].to_broadcast([P, n, width * D])

        def relu_layernorm(dve, link, c, before):
            xc = chunk(x, c)
            mean, var, rstd = stat[:, 0, :], stat[:, 1, :], stat[:, 2, :]
            link(nc.vector.tensor_reduce(mean, xc, AX.X, ALU.add))
            link(nc.vector.scalar_tensor_tensor(v3(work[:, 0, :]), mean[:, :, None].to_broadcast([P, CB, D]), -1.0 / D, xc,
                                                ALU.mult, ALU.add))
            link(nc.vector.tensor_tensor(work[:, 1, :], work[:, 0, :], work[:, 0, :], ALU.mult))
            link(nc.vector.tensor_reduce(var, v3(work[:, 1, :]), AX.X, ALU.add))
            link(nc.vector.tensor_scalar(var, var, 1.0 / D, EPS, ALU.mult, ALU.add))
            dve.sem_inc(s_var, 1)
            dve.wait_ge(s_rstd, c + before + 1)
            link(nc.vector.reciprocal(rstd, rstd))
            link(nc.vector.scalar_tensor_tensor(v3(hc[:, :]), v3(work[:, 0, :]), 0.0, rstd[:, :, None].to_broadcast([P, CB, D]),
                                                ALU.max, ALU.mult))

        def root_of_var(act, c, before):
            act.wait_ge(s_var, c + before + 1)
            nc.scalar.activation(stat[:, 2, :], stat[:, 1, :], ACT.Sqrt).then_inc(s_rstd, 1)

        def dis_of(c):
            return dis[:, bass.ds(CB * c, CB)][:, :, None].to_broadcast([P, CB, D])

        def turn_pairs(of):
            for p in range(PAIRS):
                mm = nc.tensor.transpose(psum[p // 4][:, (p % 4) * P:(p % 4 + 1) * P], of[:, p * P:(p + 1) * P], ident[:, :])
            return mm

        def copy_turned(fn=ACT.Copy):
            nc.scalar.activation(ht[:, 0:512], psum[0][:, :], fn)
            return nc.scalar.activation(ht[:, 512:CB * D], psum[1][:, 0:CB * D - 512], fn)

        def times_pairs(w, start=True, stop=True, of=ht):
            for p in range(PAIRS):
                mm = nc.tensor.matmul(psum[2 + p // 4][:, (p % 4) * P:(p % 4 + 1) * P], of[:, p * P:(p + 1) * P],
                                      pair_w[:, PAIR_W[w], :, :], start=start and p % 4 == 0, stop=stop, skip_group_check=True)
            return mm

        def times_wide(w):
            for p in range(PAIRS):
                mm = nc.tensor.matmul(psum[2 + p // 2][:, (p % 2) * WIN:(p % 2 + 1) * WIN], ht[:, p * P:(p + 1) * P],
                                      wide_w[:, WIDE_W[w], :, :], start=True, stop=True)
            return mm

        NARROW = [(2, 0, 8), (3, 8, CB - 8)]
        WIDE = [(2, 0, 4), (3, 4, 4), (4, 8, 4), (5, 12, 2)]

        def overlap_chunks(dve, prepare, finish):
            prepare(0)
            dve.sem_inc(s_hc, 1)
            with dve.Fori(0, CHUNKS - 1) as c:
                prepare(c + 1)
                finish(c)
                dve.sem_inc(s_hc, 1)
            finish(CHUNKS - 1)

        s_hc, s_turned, s_ht = sem("s_hc"), sem("s_turned"), sem("s_ht")
        s_conv_link, s_conv_product = sem("s_conv_link"), sem("s_conv_product")
        s_conv_made, s_conv_table = sem("s_conv_made"), sem("s_conv_table")

        class Pass:
            def __init__(self, n, at=0):
                self.at = at
                self.s_rows = [sem(n + f"rows{i}") for i in range(SLOTS)]
                self.s_staged = sem(n + "staged")
                self.s_onehot = sem(n + "onehot")
                self.s_summed = sem(n + "summed")
                self.s_added = sem(n + "added")

        class Layer(Pass):
            def __init__(self, n, at=0):
                super().__init__(n, at)
                self.s_link, self.s_acc = sem(n + "link"), sem(n + "acc")
                self.s_made = sem(n + "made")
                self.s_table = sem(n + "table")
                self.s_slink, self.s_plink = sem(n + "slink"), sem(n + "plink")
                self.s_onehot_turned = sem(n + "oht")
                self.s_turned_copied = sem(n + "ohc")
                self.s_message = sem(n + "mes")

        def write_table(sp, s_made, s_table, table, of, at=0):
            with sp.Fori(0, CHUNKS) as c:
                sp.wait_ge(s_made, c + at + 1)
                sp.dma_start(table[:, bass.ds(CB * c, CB), :], of(c)).then_inc(s_table, 16)

        def sum_edges(pe, s, step, message, width):
            pe.wait_ge(s.s_added, step.n + step.back)

            def block(c):
                for j in range(G):
                    mm = nc.tensor.matmul(psum[4 + step.par][:, c * width:(c + 1) * width],
                                          onehot[:, step.slot, j, c * P:(c + 1) * P], message(j),
                                          start=(j == 0), stop=(j == G - 1), skip_group_check=True)
                return mm

            on_second(pe, step, lambda: block(1))
            block(0).then_inc(s.s_summed, 1)

        def onehot_stage(dve, s):
            def stage(step):
                dve.wait_ge(s.s_summed, step.n + step.back * (SLOTS - 1))
                on_blocks(dve, step, lambda blocks: build_onehot(step, blocks).then_inc(s.s_onehot, 1))

            return stage

        def conv_vector(dve, k, s):
            LINKS = NORM_LINKS if k == 0 else 2

            def prepare(c):
                dve.wait_ge(s_turned, c + s.at + 1)
                link = Link(dve, s_conv_link, c * LINKS + (CHUNKS * (NORM_LINKS + 2 * (k - 1)) if k else 0))
                if k == 0:
                    relu_layernorm(dve, link, c, 0)
                else:
                    link(nc.vector.tensor_tensor(v3(hc[:, :]), chunk(acc, c), dis_of(c), ALU.mult))
                    link(nc.vector.tensor_tensor(v3(hc[:, :]), v3(hc[:, :]), vector_of(f"L0_gnn_b{k}", CB), ALU.add))

            def finish(c):
                dve.wait_ge(s_conv_product, c + s.at + 1)
                for bank, b, n in NARROW:
                    ins = nc.vector.tensor_tensor(acc[:, bass.ds(CB * c + b, n), 0:D], v3(psum[bank][:, 0:n * D]),
                                                  dis[:, bass.ds(CB * c + b, n)][:, :, None].to_broadcast([P, n, D]), ALU.mult)
                ins.then_inc(s_conv_made, 1)
                dve.wait_ge(s_conv_made, c + s.at + 1)

            overlap_chunks(dve, prepare, finish)
            dve.wait_ge(s_conv_made, s.at + CHUNKS)
            dve.sem_inc(s.s_summed, SLOTS)
            dve.sem_inc(s.s_added, 2)
            dve.wait_ge(s_conv_table, 16 * (s.at + CHUNKS))

            def add_sums(step):
                dve.wait_ge(s.s_summed, step.n + SLOTS)
                dve.wait_ge(s.s_added, step.n + 1)
                to = acc[:, bass.ds(step.window, 2), 0:D]
                nc.vector.tensor_tensor(to, to, v3(psum[4 + step.par][:, 0:2 * D]), ALU.add).then_inc(s.s_added, 1)

            edge_pass(dve, [(onehot_stage(dve, s), 0), (add_sums, 2)])

        def conv_scalar(act, k, s):
            if k == 0:
                act.wait_ge(s_degrees, 1)
                nc.scalar.activation(dis[:, :], dis[:, :], ACT.Sqrt).then_inc(s_dis, 1)
            with act.Fori(0, CHUNKS) as c:
                if k == 0:
                    root_of_var(act, c, 0)
                act.wait_ge(s_turned, c + s.at + 2)
                copy_turned(ACT.Relu).then_inc(s_ht, 1)
            edge_pass(act, [(stage_rows(act, s.s_rows, s.s_staged), -SLOTS)])

        def conv_tensor(pe, k, s):
            with pe.Fori(0, CHUNKS) as c:
                pe.wait_ge(s_hc, c + s.at + 1)
                turn_pairs(hc).then_inc(s_turned, 1)
                pe.wait_ge(s_ht, c + s.at + 1)
                times_pairs(f"L0_gnn_W{k + 1}").then_inc(s_conv_product, 1)

            def sums(step):
                pe.wait_ge(s.s_onehot, step.n)
                pe.wait_ge(s.s_rows[step.slot], 16 * G * step.fill)
                sum_edges(pe, s, step, lambda j: rows[:, step.slot, j, 0:D], D)

            edge_pass(pe, [(sums, 0)])

        def conv_end_vector(dve):
            with dve.Fori(0, CHUNKS) as c:
                link = Link(dve, s_conv_link, c * 3 + CHUNKS * (NORM_LINKS + 6))
                link(nc.vector.tensor_tensor(v3(hc[:, :]), chunk(acc, c), dis_of(c), ALU.mult))
                link(nc.vector.tensor_tensor(v3(hc[:, :]), v3(hc[:, :]), vector_of("L0_gnn_b4", CB), ALU.add))
                link(nc.vector.tensor_tensor(chunk(x, c), chunk(x, c), v3(hc[:, :]), ALU.add))


        def load_features(sp, attrs, s_feats, s_used):
            f = attrs.shape[1]

            def load(at, slot, n, back=0):
                sp.wait_ge(s_used, n + back)
                sp.dma_start(feats[:, slot, :, :].rearrange("p j f -> p (j f)")[:, 0:G * f],
                             attrs[bass.ds(at, GE), :].rearrange("(p j) f -> p (j f)", j=G)).then_inc(s_feats[slot], 16)

            with sp.Fori(0, FULL // SLOTS) as i:
                for u in range(SLOTS):
                    load((SLOTS * i + u) * GE, u, SLOTS * i + u + 1)
            for g in range(FULL // SLOTS * SLOTS, NG):
                load(g * GE if g < FULL else EDGES - GE, g % SLOTS, g + 1)

            def again(step):
                n = sp.snap(step.n)
                with sp.If(step.group < FULL):
                    load(step.group.with_bounds(min_val=0, max_val=FULL - 1) * GE, 0, n, SLOTS - 1)
                with sp.If(step.group > FULL - 1):
                    load(EDGES - GE, 0, n, SLOTS - 1)
                take_waits(sp)

            beyond(sp, again)

        scratch = work[:, :, :].rearrange("p a f -> p (a f)")
        pre = [scratch[:, 0:512], scratch[:, 512:1024]]
        message = [hc[:, i * G * (D + 1):(i + 1) * G * (D + 1)].rearrange("p (j f) -> p j f", f=D + 1) for i in range(2)]
        swish = ht[:, 0:512]
        product = scratch[:, 1024:1280]
        feats_t = [scratch[:, 1280:1536], scratch[:, 1536:1792]]
        turned = [psum[i][:, :].bitcast(BF16).rearrange("p (c e) -> p c e", c=2) for i in range(2)]
        tiny = hc[:, 2 * G * (D + 1):2 * G * (D + 1) + 256]
        assert 2 * G * (D + 1) + 256 <= CB * D

        def keep_busy(n, bank):
            for i in range(n):
                nc.tensor.matmul(psum[bank][:, 0:4 * P], zeros16[:, :], zeros16[:, None, :].to_broadcast([P, 4, P]), start=True,
                                 stop=True, skip_group_check=True)

        def turn_onehot(pe, s, step):
            pe.wait_ge(s.s_onehot, step.n)
            pe.wait_ge(s.s_turned_copied, step.n + step.back)

            def block(c):
                for j in range(G):
                    half = onehot[:, step.slot, j, c * P:(c + 1) * P].bitcast(BF16)[:, 1:WIN:2]
                    mm = nc.tensor.transpose(turned[step.par][:, c, j * P:(j + 1) * P], half, ident16)
                return mm

            on_second(pe, step, lambda: block(1))
            return block(0)

        def add_scaled(dve, s, step, coef, width):
            dve.wait_ge(s.s_summed, step.n + SLOTS)
            dve.wait_ge(s.s_added, step.n + 1)

            def block(c):
                to = acc[:, bass.ds(step.window + c, 1), 0:width].rearrange("p b f -> p (b f)")
                return nc.vector.scalar_tensor_tensor(to, to, coef[:, c:c + 1],
                                                      psum[4 + step.par][:, c * width:(c + 1) * width], ALU.mult, ALU.add)

            take_waits(dve)
            on_second(dve, step, lambda: block(1))
            block(0).then_inc(s.s_added, 1)

        class Messages(Layer):
            def __init__(self, n, at=0):
                super().__init__(n, at)
                self.s_product = sem(n + "product")
                self.s_kept, self.s_read = sem(n + "kept"), sem(n + "read")
                self.s_feats = [sem(n + f"feats{i}") for i in range(SLOTS)]
                self.s_feats_turned = sem(n + "ft")
                self.s_feats_copied = sem(n + "fc")
                self.s_projected = sem(n + "pro")
                self.s_rows_used = sem(n + "use")
                self.s_tanh = sem(n + "tanh")
                self.s_side = sem(n + "side")
                self.s_act_side = sem(n + "aside")
                self.s_logits = sem(n + "log")
                self.s_top_turned = sem(n + "tt")
                self.s_top = sem(n + "top")
                self.s_top_spread = sem(n + "ts")
                self.s_weighted = sem(n + "wei")
                self.s_upd_dve, self.s_upd_pe, self.s_upd_act = sem(n + "ud"), sem(n + "up"), sem(n + "ua")
                self.s_sum, self.s_last, self.s_act_link = sem(n + "sum"), sem(n + "last"), sem(n + "alink")

        def messages():
            s = Messages("msg_", CHUNKS * (4 * (0 in layers)))
            staging = rows[:, :, :, :].rearrange("p a j f -> p (a j f)")[:, 0:CB * 2 * D]
            logits = [tiny[:, G * i:G * i + G] for i in range(2)]
            peak = [tiny[:, 8 + i:9 + i] for i in range(2)]
            top = tiny[0:1, 10:11]
            minus_top = [tiny[:, 12 + i:13 + i] for i in range(2)]
            coef = [tiny[:, 16 + 2 * i:18 + 2 * i] for i in range(2)]
            outside = [tiny[:, 24 + G * i:24 + G * i + G] for i in range(2)]
            offset = [tiny[:, 32 + G * i:32 + G * i + G] for i in range(2)]
            row_peak = tiny[0:1, 40:41]
            blocks = tiny[:, 48:48 + NBW]
            total = tiny[:, 160:162]

            def sync(sp):
                write_table(sp, s.s_made, s.s_table, tables[4], lambda c: v3(staging, 2 * D))
                load_features(sp, io["edge_attr_32"], s.s_feats, s.s_feats_turned)

            def gpsimd(pool):
                pool.wait_ge(s.s_table, 16 * (CHUNKS + 1))
                gather_pass(pool, tables[4], 2 * D, s.s_rows, s.s_rows_used, s.s_staged)

            def vector(dve):
                before = norms_before(1)
                dve.sem_inc(s.s_table, 16)
                first = Link(dve, s.s_acc)
                first(nc.vector.memset(acc[:, :, :], 0.0))

                def prepare(c):
                    dve.wait_ge(s_turned, c + s.at + 1)
                    link = Link(dve, s.s_link, c * (NORM_LINKS + 1))
                    relu_layernorm(dve, link, c, before)
                    link(nc.vector.tensor_copy(chunk(h, c), v3(hc[:, :])))

                def finish(c):
                    dve.wait_ge(s.s_product, 2 * c + 1)
                    for bank, b, n in WIDE:
                        ins = nc.vector.tensor_tensor(big[:, bass.ds(CB * c + b, n), :], v3(psum[bank][:, 0:n * 2 * D], 2 * D),
                                                      vector_of("L1_gnn_b1", n, 2), ALU.add)
                    ins.then_inc(s.s_kept, 1)

                overlap_chunks(dve, prepare, finish)
                dve.wait_ge(s.s_kept, CHUNKS)
                dve.wait_ge(s.s_table, 16 * (CHUNKS + 1))
                first(nc.vector.memset(blocks, -HUGE))
                first(nc.vector.memset(top, -HUGE))
                for credited, n in ((s.s_summed, SLOTS), (s.s_added, 2), (s.s_turned_copied, 2), (s.s_feats_turned, SLOTS),
                                    (s.s_feats_copied, 1), (s.s_projected, 2), (s.s_rows_used, SLOTS), (s.s_logits, 2),
                                    (s.s_weighted, 2), (s.s_message, 2), (s.s_top_spread, 1)):
                    dve.sem_inc(credited, n)

                def complete(step):
                    dve.wait_ge(s.s_rows[step.slot], 16 * G * step.fill)
                    dve.wait_ge(s.s_projected, step.n + 2)
                    dve.wait_ge(s.s_message, step.n + step.back)
                    nc.vector.tensor_tensor(v3(pre[step.par], 2 * D), rows[:, step.slot, :, :],
                                            v3(psum[2 + step.par][:, :], 2 * D), ALU.add).then_inc(s.s_rows_used, 1)

                def logit(step):
                    dve.wait_ge(s.s_tanh, step.n)
                    dve.wait_ge(s.s_side, step.n)
                    dve.wait_ge(s.s_weighted, step.n + step.back)
                    link = Link(dve, s.s_plink, 4 * (step.n - 1))
                    v = pre[step.par]
                    link(nc.vector.scalar_tensor_tensor(v, swish, 1.0, v, ALU.add, ALU.mult))
                    l = logits[step.par]
                    link(nc.vector.tensor_tensor(v3(product), v3(v, 2 * D)[:, :, D:2 * D],
                                                 vector_of("L1_gnn_Wa2", G), ALU.mult))
                    link(nc.vector.tensor_reduce(l, v3(product), AX.X, ALU.add))
                    link(nc.vector.scalar_tensor_tensor(l, l, 0.5, offset[step.par], ALU.mult, ALU.add))
                    nc.vector.tensor_reduce(peak[step.par], l, AX.X, ALU.max).then_inc(s.s_logits, 1)

                def raise_top(step):
                    dve.wait_ge(s.s_top_turned, step.n)
                    dve.wait_ge(s.s_top_spread, step.n)
                    link = Link(dve, s.s_slink, 2 * (step.n - 1))
                    link(nc.vector.tensor_reduce(row_peak, psum[7][0:1, 0:P], AX.X, ALU.max))
                    link(nc.vector.tensor_tensor(top, top, row_peak, ALU.max))
                    dve.sem_inc(s.s_top, 1)

                def weigh(step):
                    dve.wait_ge(s.s_weighted, step.n + 2)
                    m = message[step.par]
                    nc.vector.tensor_tensor(m[:, :, 0:D], v3(pre[step.par], 2 * D)[:, :, 0:D],
                                            m[:, :, D:D + 1].to_broadcast([P, G, D]), ALU.mult).then_inc(s.s_message, 1)

                def add_sums(step):
                    add_scaled(dve, s, step, coef[step.par], D + 1)

                make = onehot_stage(dve, s)
                edge_pass(dve, [(make, 0), (logit, 2), (weigh, 3), (complete, 1), (raise_top, 2), (add_sums, 3)],
                          serial=[make, complete, logit, raise_top, weigh, add_sums], skips=True)

                first(nc.vector.memset(total, 0.0))
                dve.sem_inc(s.s_upd_dve, 1)
                dve.wait_ge(s.s_upd_act, 1)
                final = work[:, 0, 0:NBW]
                per_block = work[:, 1, 0:NBW]
                first(nc.vector.tensor_tensor(per_block, acc[:, :, D:D + 1].rearrange("p b a -> p (b a)"), final, ALU.mult))
                first(nc.vector.tensor_reduce(total[:, 0:1], per_block, AX.X, ALU.add))
                dve.sem_inc(s.s_sum, 1)
                dve.wait_ge(s.s_sum, 2)
                first(nc.vector.reciprocal(total[:, 0:1], psum[7][:, 0:1]))
                first(nc.vector.tensor_scalar(dis[:, :], final[:, 0:NB], total[:, 0:1], None, ALU.mult))
                dve.sem_inc(s.s_sum, 1)
                for w in ("L1_gnn_W2", "L1_gnn_Wu2"):
                    first(nc.vector.tensor_scalar(pair_w[:, PAIR_W[w]], pair_w[:, PAIR_W[w]], 0.5, None, ALU.mult))
                wide, share = work[:, 0, :], stat[:, 0, :]
                with dve.Fori(0, CHUNKS) as c:
                    link = Link(dve, s.s_link, CHUNKS * (NORM_LINKS + 1) + 8 * c)

                    def banks(k, out, more):
                        dve.wait_ge(s.s_upd_pe, UPD_PE * c + k)
                        for bank, b, n in NARROW:
                            ins = nc.vector.tensor_tensor(v3(out)[:, b:b + n, :], v3(psum[bank][:, 0:n * D]), more(b, n), ALU.add)
                        link(ins)

                    link(nc.vector.tensor_tensor(v3(hc[:, :]), chunk(acc, c), dis_of(c), ALU.mult))
                    dve.sem_inc(s.s_upd_dve, 1)
                    link(nc.vector.tensor_tensor(share, acc[:, bass.ds(CB * c, CB), D:D + 1].rearrange("p b a -> p (b a)"),
                                                 dis[:, bass.ds(CB * c, CB)], ALU.mult))
                    link(nc.vector.tensor_tensor(v3(wide), vector_of("L1_gnn_b2", CB), share[:, :, None].to_broadcast([P, CB, D]),
                                                 ALU.mult))
                    banks(2, hc[:, :], lambda b, n: v3(wide)[:, b:b + n, :])
                    dve.sem_inc(s.s_upd_dve, 1)
                    banks(6, wide, lambda b, n: vector_of("L1_gnn_bu1", n))
                    dve.sem_inc(s.s_upd_dve, 1)
                    dve.wait_ge(s.s_upd_act, UPD_ACT * c + 6)
                    link(nc.vector.scalar_tensor_tensor(hc[:, :], work[:, 1, :], 1.0, wide, ALU.add, ALU.mult))
                    dve.sem_inc(s.s_upd_dve, 1)
                    banks(8, wide, lambda b, n: vector_of("L1_gnn_bu2", n))
                    link(nc.vector.tensor_tensor(chunk(x, c), chunk(x, c), v3(wide), ALU.add))

            UPD_PE, UPD_ACT = 8, 6

            def scalar(act):
                before = norms_before(1)

                def turned_chunk(c):
                    act.wait_ge(s_turned, c + s.at + 2)
                    copy_turned().then_inc(s_ht, 1)

                def read_senders(c):
                    act.wait_ge(s.s_product, 2 * c + 2)
                    act.wait_ge(s.s_table, 16 * (c + 1))
                    for bank, b, n in WIDE:
                        ins = nc.scalar.activation(staging[:, b * 2 * D:(b + n) * 2 * D], psum[bank][:, 0:n * 2 * D], ACT.Copy)
                    ins.then_inc(s.s_made, 1)
                    act.wait_ge(s.s_made, c + 1)
                    act.sem_inc(s.s_read, 1)

                root_of_var(act, 0, before)
                with act.Fori(0, CHUNKS - 1) as c:
                    turned_chunk(c)
                    root_of_var(act, c + 1, before)
                    read_senders(c)
                turned_chunk(CHUNKS - 1)
                read_senders(CHUNKS - 1)

                def copy_onehot(step):
                    act.wait_ge(s.s_onehot_turned, step.n)
                    act.wait_ge(s.s_projected, step.n + step.back)
                    on_blocks(act, step, lambda blocks: nc.scalar.activation(
                        onehot_t[:, step.par, 0:blocks, :], turned[step.par][:, 0:blocks, :], ACT.Copy)
                        .then_inc(s.s_turned_copied, 1))

                def copy_feats(step):
                    act.wait_ge(s.s_feats_turned, step.n + SLOTS)
                    nc.scalar.activation(feats_t[step.par][:, 0:P], psum[6][:, 0:P], ACT.Copy).then_inc(s.s_feats_copied, 1)

                def tanhs(step):
                    act.wait_ge(s.s_rows_used, step.n + SLOTS)
                    act.wait_ge(s.s_logits, step.n + 1)
                    nc.scalar.activation(swish[:, :], pre[step.par], ACT.Tanh, scale=0.5).then_inc(s.s_tanh, 1)

                def sides(step):
                    act.wait_ge(s.s_logits, step.n + step.back)
                    take_waits(act)
                    link = Link(act, s.s_act_side, 2 * (step.n - 1))
                    out = outside[step.par]
                    link(nc.scalar.activation(out, dst_of(step.group), ACT.Abs, bias=from_middle[:, bass.ds(step.window, 1)]))
                    link(nc.scalar.activation(out, out, ACT.Relu, bias=minus_half[:, 0:1]))
                    nc.scalar.activation(offset[step.par], out, ACT.Identity, bias=consts[:, 1:2],
                                         scale=-HUGE).then_inc(s.s_side, 1)

                def exps(step):
                    act.wait_ge(s.s_top_spread, step.n + 1)
                    act.wait_ge(s.s_added, step.n + step.back)
                    act.wait_ge(s.s_summed, step.n + 2 + step.back)
                    link = Link(act, s.s_act_link, 3 * (step.n - 1))
                    m = minus_top[step.par]
                    link(nc.scalar.activation(m, psum[7][:, P:P + 1], ACT.Copy, scale=-1.0))
                    take_waits(act)

                    def rescale(n):
                        at = blocks[:, bass.ds(step.window, n)]
                        nc.scalar.activation(coef[step.par][:, 0:n], at, ACT.Exp, bias=m).then_inc(s.s_act_link, 1)
                        act.wait_ge(s.s_act_link, 3 * step.n - 1)
                        take_waits(act)
                        nc.scalar.activation(at, psum[7][:, P:P + 1].to_broadcast([P, n]), ACT.Copy).then_inc(s.s_act_link, 1)

                    on_blocks(act, step, rescale)
                    act.wait_ge(s.s_act_link, 3 * step.n)
                    nc.scalar.activation(message[step.par][:, :, D:D + 1].rearrange("p j a -> p (j a)"), logits[step.par], ACT.Exp,
                                         bias=m).then_inc(s.s_weighted, 1)

                stage = stage_rows(act, s.s_rows, s.s_staged)
                edge_pass(act, [(copy_onehot, 0), (copy_feats, 0), (sides, 1), (tanhs, 1), (stage, -SLOTS), (exps, 2)],
                          serial=[stage, copy_onehot, copy_feats, sides, tanhs, exps], skips=True)
                act.wait_ge(s.s_upd_dve, 1)
                nc.scalar.activation(minus_top[0], psum[7][:, P:P + 1], ACT.Copy, scale=-1.0).then_inc(s.s_last, 1)
                act.wait_ge(s.s_last, 1)
                nc.scalar.activation(work[:, 0, 0:NBW], blocks, ACT.Exp, bias=minus_top[0]).then_inc(s.s_upd_act, 1)
                act.wait_ge(s.s_sum, 3)
                with act.Fori(0, CHUNKS) as c:
                    def pe_event(k):
                        act.wait_ge(s.s_upd_pe, UPD_PE * c + k)

                    act.wait_ge(s.s_upd_dve, 4 * c + 1)
                    nc.scalar.activation(v3(work[:, 1, :]), chunk(h, c), ACT.Copy).then_inc(s.s_upd_act, 1)
                    pe_event(1)
                    copy_turned().then_inc(s.s_upd_act, 1)
                    pe_event(3)
                    copy_turned().then_inc(s.s_upd_act, 1)
                    pe_event(5)
                    copy_turned().then_inc(s.s_upd_act, 1)
                    act.wait_ge(s.s_upd_dve, 4 * c + 4)
                    nc.scalar.activation(work[:, 1, :], work[:, 0, :], ACT.Tanh, scale=0.5).then_inc(s.s_upd_act, 1)
                    pe_event(7)
                    copy_turned().then_inc(s.s_upd_act, 1)

            def tensor(pe):
                pe.sem_inc(s.s_read, 1)
                with pe.Fori(0, CHUNKS) as c:
                    pe.wait_ge(s_hc, c + s.at + 1)
                    turn_pairs(hc).then_inc(s_turned, 1)
                    pe.wait_ge(s_ht, c + s.at + 1)
                    pe.wait_ge(s.s_read, c + 1)
                    times_wide("receiver").then_inc(s.s_product, 1)
                    pe.wait_ge(s.s_kept, c + 1)
                    times_wide("sender").then_inc(s.s_product, 1)

                def turn(step):
                    turn_onehot(pe, s, step).then_inc(s.s_onehot_turned, 1)

                def turn_feats(step):
                    pe.wait_ge(s.s_feats[step.slot], 16 * step.fill)
                    pe.wait_ge(s.s_feats_copied, step.n)
                    keep_busy(IDLE_PRODUCTS[1], 6)
                    nc.tensor.transpose(psum[6][:, 0:P], feats[:, step.slot, :, :].rearrange("p j f -> p (j f)")[:, 0:P],
                                        ident[:, :]).then_inc(s.s_feats_turned, 1)

                def project(step):
                    pe.wait_ge(s.s_turned_copied, step.n + 2)
                    pe.wait_ge(s.s_feats_copied, step.n + 1)
                    pe.wait_ge(s.s_rows_used, step.n + 2 + step.back)
                    bank = psum[2 + step.par]
                    nc.tensor.matmul(bank[:, :], feats_t[step.par][:, 0:P], edge_w[:, :, :], start=True, stop=False,
                                     skip_group_check=True)

                    def block(c):
                        at_block = big[:, bass.ds(step.window + c, 1), :].rearrange("p b f -> p (b f)")
                        for j in range(G):
                            mm = nc.tensor.matmul(bank[:, j * 2 * D:(j + 1) * 2 * D], onehot_t[:, step.par, c, j * P:(j + 1) * P],
                                                  at_block, start=False, stop=(c == 0), skip_group_check=True)
                        return mm

                    on_second(pe, step, lambda: block(1))
                    block(0).then_inc(s.s_projected, 1)

                def turn_top(step):
                    pe.wait_ge(s.s_logits, step.n + 2)
                    pe.wait_ge(s.s_weighted, step.n + 1)
                    nc.tensor.matmul(psum[7][0:1, 0:P], peak[step.par], ident[:, :], start=True, stop=True,
                                     skip_group_check=True).then_inc(s.s_top_turned, 1)

                def spread_top(step):
                    pe.wait_ge(s.s_top, step.n)
                    nc.tensor.matmul(psum[7][:, P:P + 1], ones[0:1, :], top, start=True, stop=True,
                                     skip_group_check=True).then_inc(s.s_top_spread, 1)

                def sums(step):
                    pe.wait_ge(s.s_message, step.n + 2)
                    sum_edges(pe, s, step, lambda j: message[step.par][:, j, :], D + 1)

                edge_pass(pe, [(project, 1), (turn, 0), (turn_feats, 0), (turn_top, 2), (sums, 3), (spread_top, 2)],
                          serial=[turn, turn_feats, project, turn_top, spread_top, sums], skips=True)
                pe.wait_ge(s.s_sum, 1)
                nc.tensor.matmul(psum[7][:, 0:1], ones[:, :], total[:, 0:1], start=True, stop=True).then_inc(s.s_sum, 1)
                with pe.Fori(0, CHUNKS) as c:
                    def vector_event(k):
                        pe.wait_ge(s.s_upd_dve, 4 * c + 1 + k)

                    def copied(k):
                        pe.wait_ge(s.s_upd_act, UPD_ACT * c + 1 + k)

                    def event(ins):
                        ins.then_inc(s.s_upd_pe, 1)

                    vector_event(1)
                    event(turn_pairs(hc))
                    copied(2)
                    event(times_pairs("L1_gnn_W2"))
                    vector_event(2)
                    event(turn_pairs(hc))
                    copied(3)
                    event(times_pairs("Wu1_sum", stop=False))
                    event(turn_pairs(work[:, 1, :]))
                    copied(4)
                    event(times_pairs("Wu1_node", start=False))
                    vector_event(4)
                    event(turn_pairs(hc))
                    copied(6)
                    event(times_pairs("L1_gnn_Wu2"))

            return {"sync": sync, "gpsimd": gpsimd, "vector": vector, "scalar": scalar, "tensor": tensor}

        class Head(Layer):
            def __init__(self, n, at=0):
                super().__init__(n, at)
                self.s_masks = sem(n + "mask")
                self.s_spread = sem(n + "spr")
                self.s_top = sem(n + "top")
                self.s_gathered = sem(n + "gat")
                self.s_scored = sem(n + "sco")
                self.s_weighted = sem(n + "wei")

        def head():
            s = Head("head_")
            SPREAD, GATHERED = (2, 6), (3, 7)
            W = D + 4
            staging = rows[:, :, :, :].rearrange("p a j f -> p (a j f)")[:, 0:CB * W]
            masks = [scratch[:, 0:2 * G * P], feats[:, :, :, :].rearrange("p a j f -> p (a j f)")[:, 0:2 * G * P]]
            peaks = big[:, :, 0:2]
            seg, new, drop = ([tiny[:, k + 2 * i:k + 2 * i + 2] for i in range(2)] for k in (0, 8, 16))
            coef = [tiny[:, 24 + 2 * i:26 + 2 * i] for i in range(2)]
            z, e, t = (tiny[:, k:k + G] for k in (32, 40, 48))
            to_exp = [tiny[:, 56 + G * i:56 + G * i + G] for i in range(2)]
            weights = [tiny[:, 72 + G * i:72 + G * i + G] for i in range(2)]
            now = [tiny[:, 80 + 4 * i:84 + 4 * i].rearrange("p (b a) -> p b a", a=2) for i in range(2)]

            def sync(sp):
                write_table(sp, s.s_made, s.s_table, tables[5], lambda c: v3(staging, W))

            def gpsimd(pool):
                pool.wait_ge(s.s_table, 16 * (CHUNKS + 1))
                gather_pass(pool, tables[5], W, s.s_rows, s.s_message, s.s_staged)

            def vector(dve):
                before = norms_before(2)
                dve.sem_inc(s.s_table, 16)
                first = Link(dve, s.s_acc)
                first(nc.vector.memset(acc[:, :, :], 0.0))
                first(nc.vector.memset(peaks, -HUGE))
                LINKS = NORM_LINKS + 13
                with dve.Fori(0, CHUNKS) as c:
                    link = Link(dve, s.s_link, c * LINKS)
                    relu_layernorm(dve, link, c, before)
                    dve.wait_ge(s.s_table, 16 * (c + 1))
                    to, hv = v3(staging, W), v3(hc[:, :])
                    link(nc.vector.tensor_copy(to[:, :, 0:D], hv))
                    link(nc.vector.memset(to[:, :, D:D + 1], 1.0))
                    for name, out in (("L2_source", to[:, :, D + 1:D + 2]), ("L2_dest", peaks[:, bass.ds(CB * c, CB), 0:1])):
                        link(nc.vector.tensor_tensor(v3(work[:, 0, :]), hv, vector_of(name, CB), ALU.mult))
                        out = out.rearrange("p b a -> p (b a)")
                        link(nc.vector.tensor_reduce(out, v3(work[:, 0, :]), AX.X, ALU.add))
                    rest, parts = stat[:, 0, :], to[:, :, D + 2:D + 4].bitcast(BF16)
                    link(nc.vector.tensor_copy(rest, to[:, :, D + 1:D + 2].rearrange("p b a -> p (b a)")))
                    link(nc.vector.memset(parts, 0.0))
                    for k in range(3):
                        at = parts[:, :, k:k + 1].rearrange("p b a -> p (b a)")
                        link(nc.vector.tensor_copy(at, rest))
                        if k < 2:
                            link(nc.vector.tensor_tensor(rest, rest, at, ALU.subtract))
                    dve.sem_inc(s.s_made, 1)
                dve.wait_ge(s.s_table, 16 * (CHUNKS + 1))
                scores = peaks[:, 0:NB, 0:1].rearrange("p b a -> p (b a)")
                first(nc.vector.tensor_scalar(scores, scores, consts[:, 0:1], None, ALU.add))
                for credited, n in ((s.s_summed, SLOTS), (s.s_added, 2), (s.s_turned_copied, 2), (s.s_top, 2),
                                    (s.s_gathered, 2), (s.s_scored, 2), (s.s_weighted, 2), (s.s_message, SLOTS)):
                    dve.sem_inc(credited, n)

                def raise_peaks(step):
                    dve.wait_ge(s.s_masks, step.n)
                    dve.wait_ge(s.s_spread, step.n)
                    dve.wait_ge(s.s_top, step.n + 1)
                    dve.wait_ge(s.s_gathered, step.n + step.back)
                    dve.wait_ge(s.s_weighted, step.n + step.back)
                    take_waits(dve)
                    link = Link(dve, s.s_plink, 5 * (step.n - 1))
                    g, n, d = seg[step.par], new[step.par], drop[step.par]

                    def highest(blocks):
                        for c in range(blocks):
                            part = masks[step.par][:, c * G * P:(c + 1) * G * P]
                            ins = nc.vector.tensor_tensor_reduce(part, part, psum[SPREAD[step.par]][:, :], 1.0, -4 * HUGE, ALU.add, ALU.max,
                                                                 g[:, c:c + 1])
                        if blocks == 1:
                            ins = nc.vector.memset(g[:, 1:2], -HUGE)
                        ins.then_inc(s.s_plink, 1)

                    on_blocks(dve, step, highest)
                    link.k = 1
                    dve.wait_ge(s.s_plink, link.base + 1)
                    at = peaks[:, bass.ds(step.window, 2), :]
                    own, top = (at[:, :, k:k + 1].rearrange("p b a -> p (b a)") for k in range(2))
                    link(nc.vector.tensor_tensor(g, g, own, ALU.add))
                    link(nc.vector.scalar_tensor_tensor(n, g, 0.01, g, ALU.mult, ALU.max))
                    link(nc.vector.scalar_tensor_tensor(d, n, -1.0, top, ALU.mult, ALU.add))
                    link(nc.vector.tensor_scalar(d, d, 0.0, None, ALU.min))
                    to_own, to_top = (now[step.par][:, :, k:k + 1].rearrange("p b a -> p (b a)") for k in range(2))
                    nc.vector.tensor_tensor(to_own, own, own, ALU.max)
                    nc.vector.tensor_tensor(to_top, top, n, ALU.max)
                    nc.vector.tensor_tensor(top, top, n, ALU.max).then_inc(s.s_top, 1)

                def score(step):
                    dve.wait_ge(s.s_rows[step.slot], 16 * G * step.fill)
                    dve.wait_ge(s.s_gathered, step.n + 2)
                    link = Link(dve, s.s_slink, 3 * (step.n - 1))
                    bank = psum[GATHERED[step.par]][:, 0:2 * G].rearrange("p (j a) -> p j a", a=2)
                    source = rows[:, step.slot, :, D + 1:D + 2].rearrange("p j a -> p (j a)")
                    own, top = (bank[:, :, k:k + 1].rearrange("p j a -> p (j a)") for k in range(2))
                    link(nc.vector.tensor_tensor(z, source, own, ALU.add))
                    link(nc.vector.scalar_tensor_tensor(e, z, 0.01, z, ALU.mult, ALU.max))
                    link(nc.vector.tensor_tensor(t, e, top, ALU.subtract))
                    nc.vector.tensor_scalar(to_exp[step.par], t, 0.0, None, ALU.min).then_inc(s.s_scored, 1)

                def weigh(step):
                    dve.wait_ge(s.s_weighted, step.n + 2)
                    dve.wait_ge(s.s_summed, step.n + 2 + step.back)
                    nc.vector.tensor_tensor(message[step.par], rows[:, step.slot, :, 0:D + 1],
                                            weights[step.par][:, :, None].to_broadcast([P, G, D + 1]),
                                            ALU.mult).then_inc(s.s_message, 1)

                def add_sums(step):
                    add_scaled(dve, s, step, coef[step.par], D + 1)

                make = onehot_stage(dve, s)
                edge_pass(dve, [(make, 0), (raise_peaks, 1), (score, 2), (weigh, 2), (add_sums, 3)],
                          serial=[make, raise_peaks, score, weigh, add_sums], skips=True)
                with dve.Fori(0, CHUNKS) as c:
                    link = Link(dve, s.s_link, CHUNKS * LINKS + 4 * c)
                    total = stat[:, 0, :]
                    link(nc.vector.tensor_scalar(total, chunk(acc, c, D + 1)[:, :, D:D + 1].rearrange("p b a -> p (b a)"), 1.0e-30,
                                                 None, ALU.max))
                    link(nc.vector.reciprocal(total, total))
                    link(nc.vector.tensor_tensor(v3(hc[:, :]), chunk(acc, c), total[:, :, None].to_broadcast([P, CB, D]),
                                                 ALU.mult))
                    link(nc.vector.tensor_tensor(chunk(x, c), chunk(x, c), v3(hc[:, :]), ALU.add))

            def scalar(act):
                before = norms_before(2)
                with act.Fori(0, CHUNKS) as c:
                    root_of_var(act, c, before)

                def copy_onehot(step):
                    act.wait_ge(s.s_onehot_turned, step.n)
                    act.wait_ge(s.s_top, step.n + step.back)
                    act.wait_ge(s.s_gathered, step.n + step.back)

                    def copy(blocks):
                        of = turned[step.par][:, 0:blocks, :]
                        nc.scalar.activation(masks[step.par][:, 0:blocks * G * P].rearrange("p (c e) -> p c e", e=G * P), of, ACT.Copy,
                                             bias=-HUGE, scale=HUGE).then_inc(s.s_masks, 1)
                        nc.scalar.activation(onehot_t[:, step.par, 0:blocks, :], of, ACT.Copy).then_inc(s.s_turned_copied, 1)

                    on_blocks(act, step, copy)

                def exps(step):
                    act.wait_ge(s.s_scored, step.n + 2)
                    act.wait_ge(s.s_top, step.n + 2)
                    act.wait_ge(s.s_message, step.n + 2 + step.back)
                    act.wait_ge(s.s_added, step.n + step.back)
                    nc.scalar.activation(coef[step.par], drop[step.par], ACT.Exp)
                    nc.scalar.activation(weights[step.par], to_exp[step.par], ACT.Exp).then_inc(s.s_weighted, 1)

                stage = stage_rows(act, s.s_rows, s.s_staged)
                edge_pass(act, [(exps, 2), (stage, -SLOTS), (copy_onehot, 0)], serial=[stage, copy_onehot, exps], skips=True)

            def tensor(pe):
                def turn(step):
                    turn_onehot(pe, s, step).then_inc(s.s_onehot_turned, 1)

                def spread(step):
                    pe.wait_ge(s.s_rows[step.slot], 16 * G * step.fill)
                    pe.wait_ge(s.s_top, step.n + step.back)
                    for j in range(G):
                        for k in range(3):
                            at = rows[:, step.slot, j, D + 2:D + 4].bitcast(BF16)[:, k:k + 1]
                            mm = nc.tensor.matmul(psum[SPREAD[step.par]][:, j * P:(j + 1) * P], at.to_broadcast([P, P]),
                                                  ident16, start=(k == 0), stop=(k == 2))
                    mm.then_inc(s.s_spread, 1)

                def gather(step):
                    pe.wait_ge(s.s_top, step.n + 2)
                    pe.wait_ge(s.s_turned_copied, step.n + 2)
                    pe.wait_ge(s.s_scored, step.n + step.back)
                    bank = psum[GATHERED[step.par]]
                    nc.tensor.matmul(bank[:, 0:2 * G], zeros16[:, :], zeros16[:, 0:2 * G], start=True, stop=False,
                                     skip_group_check=True)

                    def block(c):
                        for j in range(G):
                            mm = nc.tensor.matmul(bank[:, 2 * j:2 * j + 2], onehot_t[:, step.par, c, j * P:(j + 1) * P],
                                                  now[step.par][:, c, :],
                                                  start=False, stop=(c == 0), skip_group_check=True)
                        return mm

                    on_second(pe, step, lambda: block(1))
                    block(0).then_inc(s.s_gathered, 1)
                    keep_busy(IDLE_PRODUCTS[2], SPREAD[step.par])

                def sums(step):
                    pe.wait_ge(s.s_message, step.n + SLOTS)
                    sum_edges(pe, s, step, lambda j: message[step.par][:, j, :], D + 1)

                edge_pass(pe, [(turn, 0), (sums, 3), (spread, 0), (gather, 1)], serial=[turn, spread, gather, sums], skips=True)

            return {"sync": sync, "gpsimd": gpsimd, "vector": vector, "scalar": scalar, "tensor": tensor}

        class Attention(Layer):
            def __init__(self, n, at=0):
                super().__init__(n, at)
                self.s_product = sem(n + "product")
                self.s_kept = sem(n + "kept")
                self.s_feats = [sem(n + f"feats{i}") for i in range(SLOTS)]
                self.s_feats_turned = sem(n + "ft")
                self.s_feats_copied = sem(n + "fc")
                self.s_gathered = sem(n + "gat")
                self.s_scored = sem(n + "sco")
                self.s_weighted = sem(n + "wei")

        def attention():
            s = Attention("att_", CHUNKS * (4 * (0 in layers) + (1 in layers)))
            staging = rows[:, :, :, :].rearrange("p a j f -> p (a j f)")[:, 0:CB * 2 * D]
            scores = [tiny[:, i * 64:i * 64 + G * HEADS] for i in range(2)]
            weights = [tiny[:, 128 + i * 64:128 + i * 64 + G * HEADS] for i in range(2)]

            def sync(sp):
                write_table(sp, s.s_made, s.s_table, tables[6], lambda c: v3(staging, 2 * D))
                load_features(sp, io["edge_attr_64"], s.s_feats, s.s_feats_turned)

            def gpsimd(pool):
                pool.wait_ge(s.s_table, 16 * (CHUNKS + 1))
                gather_pass(pool, tables[6], 2 * D, s.s_rows, s.s_message, s.s_staged)

            def vector(dve):
                before = norms_before(3)
                dve.sem_inc(s.s_table, 16)
                nc.vector.memset(acc[:, :, :], 0.0).then_inc(s.s_acc, 1)

                def prepare(c):
                    dve.wait_ge(s_turned, c + s.at + 1)
                    link = Link(dve, s.s_link, c * NORM_LINKS)
                    relu_layernorm(dve, link, c, before)

                def finish(c):
                    dve.wait_ge(s.s_product, 2 * c + 1)
                    for bank, b, n in NARROW:
                        ins = nc.vector.tensor_tensor(big[:, bass.ds(CB * c + b, n), 0:D], v3(psum[bank][:, 0:n * D]),
                                                      vector_of("L3_gnn_bQ", n), ALU.add)
                    ins.then_inc(s.s_kept, 1)
                    dve.wait_ge(s.s_product, 2 * c + 2)
                    dve.wait_ge(s.s_table, 16 * (c + 1))
                    for bank, b, n in WIDE:
                        ins = nc.vector.tensor_tensor(v3(staging, 2 * D)[:, b:b + n, :], v3(psum[bank][:, 0:n * 2 * D], 2 * D),
                                                      vector_of("L3_gnn_bK", n, 2), ALU.add)
                    ins.then_inc(s.s_made, 1)
                    dve.wait_ge(s.s_made, c + 1)

                overlap_chunks(dve, prepare, finish)
                dve.wait_ge(s.s_made, CHUNKS)
                dve.wait_ge(s.s_kept, CHUNKS)
                dve.wait_ge(s.s_acc, 1)
                link = Link(dve, s.s_acc, 1)
                part16, rest = work[:, 0, 0:D // 2].bitcast(BF16), work[:, 0, D:2 * D]
                parts = work[:, 0, 2 * D:3 * D]
                link(nc.vector.tensor_copy(rest, vectors[:, VECTORS["L3_gnn_bE"], :]))
                link(nc.vector.memset(parts, 0.0))
                for k in range(3):
                    link(nc.vector.tensor_copy(part16, rest))
                    link(nc.vector.scalar_tensor_tensor(parts, part16, ident[:, k:k + 1], parts, ALU.mult, ALU.add))
                    link(nc.vector.tensor_tensor(rest, rest, part16, ALU.subtract))
                link(nc.vector.tensor_copy(bias16[:, :], parts))
                dve.wait_ge(s.s_table, 16 * (CHUNKS + 1))
                for credited, n in ((s.s_summed, SLOTS), (s.s_added, 2), (s.s_turned_copied, 2), (s.s_feats_turned, SLOTS),
                                    (s.s_feats_copied, 1), (s.s_gathered, 2), (s.s_scored, 2), (s.s_message, SLOTS)):
                    dve.sem_inc(credited, n)

                def score(step):
                    dve.wait_ge(s.s_rows[step.slot], 16 * G * step.fill)
                    dve.wait_ge(s.s_gathered, step.n + 2)
                    dve.wait_ge(s.s_weighted, step.n)
                    link = Link(dve, s.s_slink, 4 * (step.n - 1))
                    p, bank, sc = product, psum[2 + step.par], scores[step.par]
                    link(nc.vector.tensor_tensor(v3(p), rows[:, step.slot, :, 0:D], v3(bank[:, 0:G * D]), ALU.mult))
                    link(nc.vector.tensor_tensor(p, p, bank[:, G * D:2 * G * D], ALU.mult))
                    link(nc.vector.tensor_reduce(sc, p.rearrange("p (h d) -> p h d", d=D // HEADS), AX.X, ALU.add))
                    link(nc.vector.tensor_scalar(sc, sc, float((D // HEADS) ** -0.5), -5.0, ALU.mult, ALU.max))
                    nc.vector.tensor_scalar(sc, sc, 5.0, None, ALU.min).then_inc(s.s_scored, 1)

                def weigh(step):
                    dve.wait_ge(s.s_weighted, step.n + 2)
                    dve.wait_ge(s.s_summed, step.n + 2 + step.back)
                    value = rows[:, step.slot, :, D:2 * D].rearrange("p j (h d) -> p j h d", h=HEADS)
                    w = weights[step.par].rearrange("p (j h) -> p j h", h=HEADS)[:, :, :, None].to_broadcast([P, G, HEADS, D // HEADS])
                    to = message[step.par][:, :, 0:D].rearrange("p j (h d) -> p j h d", h=HEADS)
                    nc.vector.tensor_tensor(to, value, w, ALU.mult).then_inc(s.s_message, 1)

                def add_sums(step):
                    dve.wait_ge(s.s_summed, step.n + SLOTS)
                    dve.wait_ge(s.s_added, step.n + 1)

                    def add(blocks):
                        to = acc[:, bass.ds(step.window, blocks), 0:D]
                        nc.vector.tensor_tensor(to, to, v3(psum[4 + step.par][:, 0:blocks * D]), ALU.add).then_inc(s.s_added, 1)

                    on_blocks(dve, step, add)

                make = onehot_stage(dve, s)
                edge_pass(dve, [(make, 0), (score, 2), (weigh, 2), (add_sums, 3)], serial=[make, score, weigh, add_sums], skips=True)
                with dve.Fori(0, CHUNKS) as c:
                    link = Link(dve, s.s_link, CHUNKS * NORM_LINKS + c)
                    link(nc.vector.tensor_tensor(chunk(x, c), chunk(x, c), chunk(acc, c), ALU.add))

            def scalar(act):
                before = norms_before(3)
                with act.Fori(0, CHUNKS) as c:
                    root_of_var(act, c, before)
                    act.wait_ge(s_turned, c + s.at + 2)
                    copy_turned().then_inc(s_ht, 1)
                act.sem_inc(s.s_weighted, 2)

                def copy_onehot(step):
                    act.wait_ge(s.s_onehot_turned, step.n)
                    act.wait_ge(s.s_gathered, step.n + step.back)
                    on_blocks(act, step, lambda blocks: nc.scalar.activation(
                        onehot_t[:, step.par, 0:blocks, :], turned[step.par][:, 0:blocks, :], ACT.Copy)
                        .then_inc(s.s_turned_copied, 1))

                def copy_feats(step):
                    act.wait_ge(s.s_feats_turned, step.n + SLOTS)
                    nc.scalar.activation(feats_t[step.par], psum[6][:, 0:2 * P], ACT.Copy).then_inc(s.s_feats_copied, 1)

                def exps(step):
                    act.wait_ge(s.s_scored, step.n + 2)
                    act.wait_ge(s.s_message, step.n + 2 + step.back)
                    nc.scalar.activation(weights[step.par], scores[step.par], ACT.Exp).then_inc(s.s_weighted, 1)

                stage = stage_rows(act, s.s_rows, s.s_staged)
                edge_pass(act, [(exps, 2), (stage, -SLOTS), (copy_onehot, 0), (copy_feats, 0)],
                          serial=[stage, copy_onehot, copy_feats, exps], skips=True)

            def tensor(pe):
                with pe.Fori(0, CHUNKS) as c:
                    pe.wait_ge(s_hc, c + s.at + 1)
                    turn_pairs(hc).then_inc(s_turned, 1)
                    pe.wait_ge(s_ht, c + s.at + 1)
                    times_pairs("L3_gnn_WQ").then_inc(s.s_product, 1)
                    pe.wait_ge(s.s_kept, c + 1)
                    times_wide("key_value").then_inc(s.s_product, 1)

                def turn(step):
                    turn_onehot(pe, s, step).then_inc(s.s_onehot_turned, 1)

                def turn_feats(step):
                    pe.wait_ge(s.s_feats[step.slot], 16 * step.fill)
                    pe.wait_ge(s.s_feats_copied, step.n)
                    for half in range(2):
                        mm = nc.tensor.transpose(psum[6][:, half * P:(half + 1) * P],
                                                 feats[:, step.slot, 2 * half:2 * half + 2, :].rearrange("p j f -> p (j f)"),
                                                 ident[:, :])
                    mm.then_inc(s.s_feats_turned, 1)

                def gather_and_project(step):
                    pe.wait_ge(s.s_turned_copied, step.n + 2)
                    pe.wait_ge(s.s_feats_copied, step.n + 1)
                    pe.wait_ge(s.s_scored, step.n + step.back)
                    bank = psum[2 + step.par]
                    for half in range(2):
                        nc.tensor.matmul(bank[:, (2 + half) * P:(3 + half) * P], feats_t[step.par][:, half * P:(half + 1) * P],
                                         pair_w[:, PAIR_W["L3_gnn_WE"], :, :], start=(half == 0), stop=False,
                                         skip_group_check=True)
                    nc.tensor.matmul(bank[:, G * D:2 * G * D], ones16[0:3, :],
                                     bias16[0:3, None, :].to_broadcast([3, G, D]), start=False, stop=True,
                                     skip_group_check=True)

                    def block(c):
                        at_block = big[:, bass.ds(step.window + c, 1), 0:D].rearrange("p b f -> p (b f)")
                        for j in range(G):
                            mm = nc.tensor.matmul(bank[:, j * D:(j + 1) * D], onehot_t[:, step.par, c, j * P:(j + 1) * P],
                                                  at_block, start=False, stop=(c == 0), skip_group_check=True)
                        return mm

                    on_second(pe, step, lambda: block(1))
                    block(0).then_inc(s.s_gathered, 1)
                    keep_busy(IDLE_PRODUCTS[3], 7)

                def sums(step):
                    pe.wait_ge(s.s_message, step.n + SLOTS)
                    sum_edges(pe, s, step, lambda j: message[step.par][:, j, 0:D], D)

                edge_pass(pe, [(turn, 0), (turn_feats, 0), (sums, 3), (gather_and_project, 1)],
                          serial=[turn, turn_feats, gather_and_project, sums], skips=True)

            return {"sync": sync, "gpsimd": gpsimd, "vector": vector, "scalar": scalar, "tensor": tensor}

        s_x_done = sem("s_x_done")
        convs = [Pass(f"conv{k}_", CHUNKS * k) for k in range(4)] if 0 in layers else []

        def norms_before(layer):
            return CHUNKS * sum(l < layer for l in layers)

        layer_runs = [run() for l, run in ((1, messages), (2, head), (3, attention)) if l in layers]

        block = ctx.enter_context(nc.Block())

        @block.sync
        def _(sp):
            prep_sync(sp)
            weight_loads(sp)
            for k, s in enumerate(convs):
                write_table(sp, s_conv_made, s_conv_table, tables[k], lambda c: chunk(acc, c), s.at)
            for run in layer_runs:
                run["sync"](sp)
            sp.wait_ge(s_x_done, 1)
            sp.dma_start(io["out"][0:(NB - 1) * P, :].rearrange("(b p) c -> p b c", p=P), x[:, 0:NB - 1, :]).then_inc(s_out, 16)
            sp.dma_start(io["out"][(NB - 1) * P:NODES, :], x[0:LAST, NB - 1, :]).then_inc(s_out, 16)
            sp.wait_ge(s_out, 32)

        @block.gpsimd
        def _(pool):
            prep_pool(pool)
            pool.wait_ge(s_index, 1)
            for k, s in enumerate(convs):
                pool.wait_ge(s_conv_table, 16 * (s.at + CHUNKS))
                gather_pass(pool, tables[k], D, s.s_rows, s.s_summed, s.s_staged)
            for run in layer_runs:
                run["gpsimd"](pool)

        @block.vector
        def _(dve):
            nc.vector.memset(pair_w[:, :, :, :], 0.0).then_inc(s_w0, 1)
            nc.vector.memset(wide_w[:, :, :, :], 0.0).then_inc(s_w0, 1)
            nc.vector.memset(edge_w[:, :, :], 0.0).then_inc(s_w0, 1)
            nc.vector.memset(ones[:, :], 1.0)
            nc.vector.memset(big[:, NB, :], 0.0).then_inc(s_w0, 1)
            prep_vector(dve)
            dve.wait_ge(s_w, 16 * WEIGHT_LOADS)
            dve.wait_ge(s_x, 32)
            for k, s in enumerate(convs):
                conv_vector(dve, k, s)
            if convs:
                conv_end_vector(dve)
            for run in layer_runs:
                run["vector"](dve)
            dve.sem_inc(s_x_done, 1)

        @block.scalar
        def _(act):
            act.wait_ge(s_index, 1)
            for k, s in enumerate(convs):
                conv_scalar(act, k, s)
            if not convs:
                act.wait_ge(s_degrees, 1)
                nc.scalar.activation(dis[:, :], dis[:, :], ACT.Sqrt).then_inc(s_dis, 1)
            for run in layer_runs:
                run["scalar"](act)

        @block.tensor
        def _(pe):
            prep_tensor(pe)
            pe.wait_ge(s_index, 1)
            pe.wait_ge(s_w, 16 * WEIGHT_LOADS)
            pe.sem_inc(s_turned, 1)
            for k, s in enumerate(convs):
                conv_tensor(pe, k, s)
            for run in layer_runs:
                run["tensor"](pe)


_INS = ["x", "src", "dst", "edge_attr_32", "edge_attr_64",
        "L0_gnn_W1", "L0_gnn_b1", "L0_gnn_W2", "L0_gnn_b2", "L0_gnn_W3", "L0_gnn_b3", "L0_gnn_W4", "L0_gnn_b4",
        "L1_gnn_W1", "L1_gnn_b1", "L1_gnn_W2", "L1_gnn_b2", "L1_gnn_Wa1", "L1_gnn_ba1", "L1_gnn_Wa2", "L1_gnn_ba2",
        "L1_gnn_Wu1", "L1_gnn_bu1", "L1_gnn_Wu2", "L1_gnn_bu2", "L2_gnn_W", "L2_gnn_b",
        "L3_gnn_WQ", "L3_gnn_bQ", "L3_gnn_WK", "L3_gnn_bK", "L3_gnn_WE", "L3_gnn_bE", "L3_gnn_WV", "L3_gnn_bV"]
_OUTS = [((NODES, D), "float32")]


def kernel(**inputs):
    import numpy as _np
    import concourse.bacc as _bacc
    from concourse import mybir as _mybir
    from concourse.bass_utils import run_bass_kernel_spmd as _run

    nc = _bacc.Bacc("TRN2", target_bir_lowering=False, num_devices=1)
    arrays, io = {}, {}
    for name in _INS:
        a = _np.ascontiguousarray(inputs[name])
        arrays[f"in_{name}"] = a
        io[name] = nc.dram_tensor(f"in_{name}", a.shape, _mybir.dt.from_np(a.dtype), kind="ExternalInput").ap()
    shape, dtype = _OUTS[0]
    io["out"] = nc.dram_tensor("out_0", shape, _mybir.dt.from_np(_np.dtype(dtype)), kind="ExternalOutput").ap()
    gnn_program(nc, io["src"], io["dst"], io)
    r = _run(nc, [arrays], core_ids=[0])
    return r.results[0]["out_0"]
```
